# Optimizing a Trainium2 kernel written in Bass

```python
import numpy as np
import jax
import jax.numpy as jnp

def _softmax(x, axis=-1):
    return jax.nn.softmax(x, axis=axis)

def _gelu(x):
    return jax.nn.gelu(x, approximate=True)

def _silu(x):
    return jax.nn.silu(x)

def _sigmoid(x):
    return jax.nn.sigmoid(x)

def _layernorm(x, axis=-1, eps=1e-05):
    m = jnp.mean(x, axis=axis, keepdims=True)
    v = jnp.var(x, axis=axis, keepdims=True)
    return (x - m) / jnp.sqrt(v + eps)

def _scatter_add(tgt, idx, src, axis=0):
    return tgt.at[idx].add(src)

def _segment_sum(src, seg, n):
    return jax.ops.segment_sum(src, seg, n)
kernel_name = 'mk_seq_postln_d1_jaxref_r4_055dc9'

def setup_inputs(seed: int=0):
    np.random.seed(seed)
    _w = jnp.asarray

    def _L0_attn_setup():
        import math
        import jax, jax.numpy as jnp
        import numpy as np
        N_HEAD = 16
        DIM = 256
        HEAD_DIM = DIM // N_HEAD

        def _rope(x):
            t, d = (x.shape[2], x.shape[3])
            inv_freq = 1.0 / 10000.0 ** (jnp.arange(0, d, 2, dtype=jnp.float32) / d)
            freqs = jnp.arange(t, dtype=jnp.float32)[:, None] * inv_freq[None, :]
            emb = jnp.repeat(freqs, 2, axis=-1)
            cos = jnp.cos(emb).astype(x.dtype)
            sin = jnp.sin(emb).astype(x.dtype)
            x1 = x[..., ::2]
            x2 = x[..., 1::2]
            rot = jnp.stack([-x2, x1], axis=-1).reshape(x.shape)
            return x * cos + rot * sin
        key = jax.random.key(seed)
        k1, k2, k3 = jax.random.split(key, 3)
        b, t = (2, 512)
        x = jax.random.normal(k1, (b, t, DIM), dtype=jnp.float32)
        w_qkv = jax.random.normal(k2, (DIM, 3 * DIM), dtype=jnp.float32) * (1.0 / math.sqrt(DIM))
        b_qkv = jnp.zeros((3 * DIM,), dtype=jnp.float32)
        w_out = jax.random.normal(k3, (DIM, DIM), dtype=jnp.float32) * (1.0 / math.sqrt(DIM))
        b_out = jnp.zeros((DIM,), dtype=jnp.float32)
        return {'x': x, 'w_qkv': w_qkv, 'b_qkv': b_qkv, 'w_out': w_out, 'b_out': b_out}
    _L0_attn_in = _L0_attn_setup()

    def _L0_ffn_setup():
        import jax, jax.numpy as jnp
        import numpy as np
        DIM = 256
        HIDDEN = 768
        SCALE = 1.0 / 127.0

        def _dequant(w_int, dtype):
            return w_int.astype(dtype) * jnp.asarray(SCALE, dtype)
        key = jax.random.key(seed)
        k_x, k_g, k_u, k_d = jax.random.split(key, 4)
        x = jax.random.normal(k_x, (4, 512, DIM), dtype=jnp.float32)
        w_gate = jax.random.randint(k_g, (HIDDEN, DIM), -127, 128, dtype=jnp.int32)
        w_up = jax.random.randint(k_u, (HIDDEN, DIM), -127, 128, dtype=jnp.int32)
        w_down = jax.random.randint(k_d, (DIM, HIDDEN), -127, 128, dtype=jnp.int32)
        return {'x': x, 'w_gate': w_gate, 'w_up': w_up, 'w_down': w_down}
    _L0_ffn_in = _L0_ffn_setup()
    _d = {'L0_attn_x': _L0_attn_in['x'], 'L0_attn_w_qkv': _L0_attn_in['w_qkv'], 'L0_attn_b_qkv': _L0_attn_in['b_qkv'], 'L0_attn_w_out': _L0_attn_in['w_out'], 'L0_attn_b_out': _L0_attn_in['b_out'], 'L0_ffn_w_gate': _L0_ffn_in['w_gate'], 'L0_ffn_w_up': _L0_ffn_in['w_up'], 'L0_ffn_w_down': _L0_ffn_in['w_down']}
    _x0 = _d['L0_attn_x']
    _d['L0_attn_x'] = jax.random.normal(jax.random.fold_in(jax.random.key(seed), 1), (4, 2048, 256), dtype=_x0.dtype)
    del _x0
    return _d

def reference(L0_attn_x, L0_attn_w_qkv, L0_attn_b_qkv, L0_attn_w_out, L0_attn_b_out, L0_ffn_w_gate, L0_ffn_w_up, L0_ffn_w_down):

    def _L0_attn_ref(x, w_qkv, b_qkv, w_out, b_out):
        import math
        import jax, jax.numpy as jnp
        import numpy as np
        N_HEAD = 16
        DIM = 256
        HEAD_DIM = DIM // N_HEAD

        def _rope(x):
            t, d = (x.shape[2], x.shape[3])
            inv_freq = 1.0 / 10000.0 ** (jnp.arange(0, d, 2, dtype=jnp.float32) / d)
            freqs = jnp.arange(t, dtype=jnp.float32)[:, None] * inv_freq[None, :]
            emb = jnp.repeat(freqs, 2, axis=-1)
            cos = jnp.cos(emb).astype(x.dtype)
            sin = jnp.sin(emb).astype(x.dtype)
            x1 = x[..., ::2]
            x2 = x[..., 1::2]
            rot = jnp.stack([-x2, x1], axis=-1).reshape(x.shape)
            return x * cos + rot * sin
        b, t, d = x.shape
        qkv = jnp.einsum('btd,de->bte', x, w_qkv) + b_qkv
        q, k, v = jnp.split(qkv, 3, axis=-1)

        def heads(z):
            return z.reshape(b, t, N_HEAD, HEAD_DIM).transpose(0, 2, 1, 3)
        q, k, v = (heads(q), heads(k), heads(v))
        q = _rope(q)
        k = _rope(k)
        attn = jnp.einsum('bhqd,bhkd->bhqk', q, k) / math.sqrt(HEAD_DIM)
        attn = jax.nn.softmax(attn, axis=-1)
        out = jnp.einsum('bhqk,bhkd->bhqd', attn, v)
        out = out.transpose(0, 2, 1, 3).reshape(b, t, d)
        return jnp.einsum('btd,de->bte', out, w_out) + b_out

    def _L0_ffn_ref(x, w_gate, w_up, w_down):
        import jax, jax.numpy as jnp
        import numpy as np
        DIM = 256
        HIDDEN = 768
        SCALE = 1.0 / 127.0

        def _dequant(w_int, dtype):
            return w_int.astype(dtype) * jnp.asarray(SCALE, dtype)
        wg = _dequant(w_gate, x.dtype)
        wu = _dequant(w_up, x.dtype)
        wd = _dequant(w_down, x.dtype)
        gate = jnp.einsum('bsd,hd->bsh', x, wg)
        up = jnp.einsum('bsd,hd->bsh', x, wu)
        h = jax.nn.silu(gate) * up
        return jnp.einsum('bsh,dh->bsd', h, wd)
    x = L0_attn_x
    x = _layernorm(x + _L0_attn_ref(x, L0_attn_w_qkv, L0_attn_b_qkv, L0_attn_w_out, L0_attn_b_out), axis=-1)
    x = _layernorm(x + _L0_ffn_ref(x, L0_ffn_w_gate, L0_ffn_w_up, L0_ffn_w_down), axis=-1)
    return x

_drawn_inputs = setup_inputs


def setup_inputs(seed=0):
    import zlib

    import numpy as np

    out = dict(_drawn_inputs(seed))
    spreads = {'L0_attn_b_qkv': (0.0, 0.1), 'L0_attn_b_out': (0.0, 0.1)}
    factors = {}
    for name, (base, spread) in spreads.items():
        noise = np.random.default_rng([zlib.crc32(name.encode()), seed]).standard_normal(out[name].shape)
        drawn = base * np.exp(spread * noise) if base else spread * noise
        out[name] = jnp.asarray(drawn.astype(out[name].dtype))
    for name, factor in factors.items():
        out[name] = (out[name] * factor).astype(out[name].dtype)
    return out
```

```python
from contextlib import ExitStack

import numpy as np

import concourse.bass as bass
from concourse import mybir

P = 128
N_HEAD = 16
PARTS = 3
BANK = 512
EPS = 1e-5
QUANT_SCALE = 1.0 / 127.0

F32 = mybir.dt.float32
BF16 = mybir.dt.bfloat16
I32 = mybir.dt.int32
ACT = mybir.ActivationFunctionType
ALU = mybir.AluOpType
AX = mybir.AxisListType


def wait(eng, sem, value):
    if not isinstance(value, int) or value > 0:
        eng.wait_ge(sem, value)


def apart(eng, passed):
    eng.sem_inc(passed, 1)


def project(nc, t, B, T, D):
    CH = BANK
    NC = T // CH
    KD = D // P
    M = 2 * KD
    HPT = P // (D // N_HEAD)
    HD = D // N_HEAD
    swap = [p ^ 1 for p in range(32)]
    with ExitStack() as ctx:
        def sb(name, shape, dt):
            return ctx.enter_context(nc.sbuf_tensor(name, shape, dt))

        def sem(name):
            return ctx.enter_context(nc.semaphore(name))

        w_qkv = sb("w_qkv", [P, KD, 3 * D], F32)
        bias_qk = sb("bias_qk", [P, 3 * KD], F32)
        bias_v = sb("bias_v", [P, D], F32)
        cos = sb("cos", [P, T], F32)
        sin = sb("sin", [P, T], F32)
        x_t = [sb(f"x_t{i}", [P, KD, CH], F32) for i in range(2)]
        raw = [sb(f"raw{i}", [P, M, CH], F32) for i in range(2)]
        turned = [sb(f"turned{i}", [P, M, CH], F32) for i in range(2)]
        roped = [sb(f"roped{i}", [P, M, CH], F32) for i in range(2)]
        parts = [sb(f"parts{i}", [P, M, PARTS, CH], BF16) for i in range(2)]
        qk_ps = [ctx.enter_context(nc.psum_tensor(f"qk_ps{m}", [P, CH], F32)) for m in range(M)]
        v_ps = [ctx.enter_context(nc.psum_tensor(f"v_ps{n}", [P, 2, D], F32)) for n in range(2)]

        passed = sem("passed")
        weights_in = sem("weights_in")
        x_in = [sem(f"x_in{i}") for i in range(2)]
        qk_done = sem("qk_done")
        v_done = sem("v_done")
        raw_done = sem("raw_done")
        v_kept = sem("v_kept")
        swapped = sem("swapped")
        cosined = sem("cosined")
        sined = sem("sined")
        roped_done = sem("roped_done")
        part1_done = sem("part1_done")
        rest1_done = sem("rest1_done")
        part2_done = sem("part2_done")
        part3_done = sem("part3_done")
        stored = [sem(f"stored{i}") for i in range(2)]
        N_WEIGHTS = 5 * 16

        block = ctx.enter_context(nc.Block())

        @block.sync
        def _(sp):
            sp.dma_start(w_qkv[:, :, :], t["w_qkv"].rearrange("(k p) n -> p k n", p=P)).then_inc(weights_in, 16)
            sp.dma_start(bias_qk[:, :], t["b_qkv_cols"]).then_inc(weights_in, 16)

            def load(c, k):
                wait(sp, v_done, (k - 1) * 2)
                sp.dma_start(x_t[c % 2][:, :, :],
                             t["x_t"].rearrange("(k p) n -> p k n", p=P)[:, :, bass.ds(k * CH, CH)]
                             ).then_inc(x_in[c % 2], 16)

            def chunks(b, first=False):
                for c in range(NC):
                    load(c, b * NC + c)
                    if first and c == 0:
                        sp.dma_start(cos[:, :], t["cos"]).then_inc(weights_in, 16)
                        sp.dma_start(sin[:, :], t["sin"]).then_inc(weights_in, 16)
                        sp.dma_start(bias_v[:, :], bass.AP(tensor=t["b_qkv"].tensor, offset=2 * D,
                                                           ap=[[0, P], [1, D]])).then_inc(weights_in, 16)

            chunks(0, True)
            with sp.Fori(1, B) as b:
                chunks(b)

        @block.tensor
        def _(pe):
            def chunks(b, first=False):
                for c in range(NC):
                    k = b * NC + c
                    x = x_t[c % 2]
                    wait(pe, x_in[c % 2], (b * (NC // 2) + c // 2 + 1) * 16)
                    for m in range(M):
                        wait(pe, raw_done, (k - 1) * M + m + 1)
                        for kd in range(KD):
                            mm = pe.matmul(qk_ps[m][:, :], w_qkv[:, kd, m * P:(m + 1) * P], x[:, kd, :],
                                           start=kd == 0, stop=kd == KD - 1)
                        mm.then_inc(qk_done, 1)
                    for n in range(2):
                        wait(pe, v_kept, (k - 1) * 2 + n + 1)
                        for j in range(2):
                            at = (2 * n + j) * P
                            for kd in range(KD):
                                mm = pe.matmul(v_ps[n][:, j, :], x[:, kd, at:at + P], w_qkv[:, kd, 2 * D:3 * D],
                                               start=kd == 0, stop=kd == KD - 1)
                        mm.then_inc(v_done, 1)

            pe.wait_ge(weights_in, N_WEIGHTS)
            chunks(0, True)
            with pe.Fori(1, B) as b:
                chunks(b)

        @block.scalar
        def _(act):
            def store(b, c):
                k = b * NC + c
                act.wait_ge(part3_done, k + 1)
                for m in range(M):
                    to = t["q_parts"] if m < KD else t["k_parts"]
                    row = (b * N_HEAD + (m % KD) * HPT) * HD
                    to = to.rearrange("h d a n -> (h d) a n")
                    act.dma_start(to[bass.ds(row, P), :, c * CH:(c + 1) * CH],
                                  parts[c % 2][:, m, :, :]).then_inc(stored[c % 2], 16)

            def chunks(b, first=False):
                for c in range(NC):
                    k = b * NC + c
                    i = c % 2
                    for m in range(M):
                        act.wait_ge(qk_done, k * M + m + 1)
                        if m == 0:
                            wait(act, part3_done, k - 1)
                        act.activation(raw[i][:, m, :], qk_ps[m][:, :], ACT.Identity,
                                       bias=bias_qk[:, m:m + 1]).then_inc(raw_done, 1)
                    act.wait_ge(roped_done, k + 1)
                    wait(act, stored[i], (b * (NC // 2) + c // 2) * 16 * M)
                    act.activation(parts[i][:, :, 0, :], roped[i][:, :, :], ACT.Copy).then_inc(part1_done, 1)
                    act.wait_ge(rest1_done, k + 1)
                    act.activation(parts[i][:, :, 1, :], raw[i][:, :, :], ACT.Copy).then_inc(part2_done, 1)
                    if c > 0:
                        store(b, c - 1)
                    elif not first:
                        store(b - 1, NC - 1)

            act.wait_ge(weights_in, N_WEIGHTS)
            chunks(0, True)
            with act.Fori(1, B) as b:
                chunks(b)
            store(B - 1, NC - 1)
            for i in range(2):
                act.wait_ge(stored[i], B * (NC // 2) * 16 * M)

        @block.vector
        def _(dve):
            def chunks(b, first=False):
                for c in range(NC):
                    k = b * NC + c
                    i = c % 2
                    for m in range(M):
                        dve.wait_ge(raw_done, k * M + m + 1)
                        if m == 0:
                            wait(dve, roped_done, k - 1)
                        apart(dve, passed)
                        last = dve.stream_shuffle(turned[i][:, m, :], raw[i][:, m, :], swap)
                    last.then_inc(swapped, 1)
                    wait(dve, part1_done, k - 1)
                    dve.tensor_tensor(roped[i][:, :, :], raw[i][:, :, :],
                                      cos[:, c * CH:(c + 1) * CH].unsqueeze(1).broadcast_to([P, M, CH]),
                                      ALU.mult).then_inc(cosined, 1)
                    for n in range(2):
                        dve.wait_ge(v_done, k * 2 + n + 1)
                        kt = c * (CH // P) + 2 * n
                        dve.tensor_tensor(
                            t["kept"][:, bass.ds(b * N_HEAD, N_HEAD), kt:kt + 2, :].rearrange("p h k d -> p k h d"),
                            v_ps[n][:, :, :].rearrange("p k (h d) -> p k h d", d=HD),
                            bias_v[:, :].rearrange("p (h d) -> p h d", d=HD).unsqueeze(1)
                            .broadcast_to([P, 2, N_HEAD, HD]), ALU.add).then_inc(v_kept, 1)
                    dve.wait_ge(cosined, k + 1)
                    dve.wait_ge(sined, k + 1)
                    dve.tensor_tensor(roped[i][:, :, :], roped[i][:, :, :], turned[i][:, :, :],
                                      ALU.add).then_inc(roped_done, 1)
                    dve.wait_ge(roped_done, k + 1)
                    dve.wait_ge(part1_done, k + 1)
                    dve.tensor_tensor(raw[i][:, :, :], roped[i][:, :, :], parts[i][:, :, 0, :],
                                      ALU.subtract).then_inc(rest1_done, 1)

            dve.wait_ge(weights_in, N_WEIGHTS)
            chunks(0, True)
            with dve.Fori(1, B) as b:
                chunks(b)

        @block.gpsimd
        def _(pool):
            def chunks(b, first=False):
                for c in range(NC):
                    k = b * NC + c
                    i = c % 2
                    pool.wait_ge(swapped, k + 1)
                    pool.tensor_tensor(turned[i][:, :, :], turned[i][:, :, :],
                                       sin[:, c * CH:(c + 1) * CH].unsqueeze(1).broadcast_to([P, M, CH]),
                                       ALU.mult).then_inc(sined, 1)
                    pool.wait_ge(part2_done, k + 1)
                    pool.tensor_tensor(parts[i][:, :, 2, :], raw[i][:, :, :], parts[i][:, :, 1, :],
                                       ALU.subtract).then_inc(part3_done, 1)

            pool.wait_ge(weights_in, N_WEIGHTS)
            chunks(0, True)
            with pool.Fori(1, B) as b:
                chunks(b)


def attend(nc, t, B, T, D):
    HD = D // N_HEAD
    HEADS = B * N_HEAD
    HALF = T // 2
    KT = T // P
    PAIRS = KT // 2
    QC = HALF // BANK
    QT = HALF // P
    EXPS = KT * QC
    WIDE = 2 * BANK
    KW = T // WIDE
    MAXES = QT * KW
    ST = 3
    SLOTS = 4
    STACK = 6 * HD
    ROWS = STACK + PARTS
    CUTS = 4
    VM = HD + 1
    SCALE = float(HD) ** -0.5
    assert QC == 2 and KW * QT == KT and MAXES == KT
    with ExitStack() as ctx:
        def sb(name, shape, dt):
            return ctx.enter_context(nc.sbuf_tensor(name, shape, dt))

        def psum(name, shape):
            return ctx.enter_context(nc.psum_tensor(name, shape, F32))

        def sem(name):
            return ctx.enter_context(nc.semaphore(name))

        q1st = [sb(f"q1st{i}", [STACK, T], BF16) for i in range(2)]
        k1st = [sb(f"k1st{i}", [STACK, T], BF16) for i in range(2)]
        q2nd = [sb(f"q2nd{i}", [ROWS, T], BF16) for i in range(2)]
        k2nd = [sb(f"k2nd{i}", [ROWS, T], BF16) for i in range(2)]
        v_head = [sb(f"v_head{i}", [P, KT, VM], F32) for i in range(2)]
        probs = [sb(f"probs{i}", [P, 2, HALF], F32) for i in range(SLOTS)]
        tile_max = [sb(f"tile_max{i}", [P, QT, KW], F32) for i in range(2)]
        neg_max = [sb(f"neg_max{i}", [P, 32], F32) for i in range(2)]
        neg_max_t = [sb(f"neg_max_t{i}", [P, 32], F32) for i in range(2)]
        max_parts = [sb(f"max_parts{i}", [P, PARTS, 32], BF16) for i in range(2)]
        max_rest = sb("max_rest", [P, 32], F32)
        sums = [sb(f"sums{i}", [P, BANK], F32) for i in range(2)]
        odd = [sb(f"odd{i}", [P // 2, BANK], F32) for i in range(2)]
        whole = [sb(f"whole{i}", [P // 2, BANK], F32) for i in range(2)]

        st_ps = [psum(f"st_ps{i}", [P, BANK]) for i in range(ST)]
        s_ps = [psum(f"s_ps{i}", [P, WIDE]) for i in range(2)]
        o_ps = psum("o_ps", [P, BANK])

        passed_sp, passed_pool = sem("passed_sp"), sem("passed_pool")
        ones_set = sem("ones_set")
        o_cleared = sem("o_cleared")
        first_in = [sem(f"first_in{i}") for i in range(2)]
        second_in = [sem(f"second_in{i}") for i in range(2)]
        max_in = [sem(f"max_in{i}") for i in range(4)]
        max_out = [sem(f"max_out{i}") for i in range(2)]
        v_ready = sem("v_ready")
        s_done = sem("s_done")
        s_read = sem("s_read")
        unit_max = sem("unit_max")
        max_turned = sem("max_turned")
        max_cut = sem("max_cut")
        cleared = sem("cleared")
        st_done = sem("st_done")
        exp_done = sem("exp_done")
        pv_done = sem("pv_done")
        sums_out = sem("sums_out")
        odd_in = [sem(f"odd_in{i}") for i in range(2)]
        whole_done = sem("whole_done")
        kept = [sem(f"kept{i}") for i in range(2)]

        def each_head(eng, body):
            def turn(i, first, last):
                body(i, 0, first, False)
                body(i, 1, False, last)
            turn(0, True, False)
            with eng.Fori(1, HEADS // 2 - 1) as i:
                turn(i, False, False)
            turn(HEADS // 2 - 1, False, True)

        def before(e, ring):
            return e - ring if e >= ring else max(j for j in range(EXPS) if j % ring == e) - EXPS

        block = ctx.enter_context(nc.Block())

        @block.sync
        def _(sp):
            def stacks(h, q_to, k_to, landed):
                def rows(parts, part, n, step):
                    head = parts[bass.ds(h, 1), :, :, :]
                    return bass.AP(tensor=head.tensor, offset=head.offset + part * T,
                                   ap=[[step, n], [PARTS * T, HD], [1, T]])
                at = 0
                for part, n in ((0, 3), (1, 2), (2, 1)):
                    sp.dma_start(q_to[at:at + n * HD, :], rows(t["q_parts"], part, n, 0)).then_inc(landed, 16)
                    at += n * HD
                at = 0
                for n in (3, 2, 1):
                    sp.dma_start(k_to[at:at + n * HD, :], rows(t["k_parts"], 0, n, T)).then_inc(landed, 16)
                    at += n * HD

            def maxima(h, hh, a):
                sp.wait_ge(max_cut, CUTS * (2 * h + a + 1))
                apart(sp, passed_sp)
                wait(sp, st_done, (2 * (h - 2) + a + 1) * EXPS)
                four = 2 * hh + a
                there = t["max_parts"][four]
                sp.dma_start(there, max_parts[a][:, :, :]).then_inc(max_out[a], 16)
                sp.wait_ge(max_out[a], (h + 1) * 16)
                for part in range(PARTS):
                    rows = bass.AP(tensor=there.tensor, offset=there.offset + part * 32,
                                   ap=[[PARTS * 32, QT], [32 * PARTS * 32, P // 32], [1, 32]])
                    sp.dma_start(q2nd[hh][STACK + part:STACK + part + 1, a * HALF:(a + 1) * HALF], rows
                                 ).then_inc(max_in[four], 16)

            def odd_rows(h, a):
                u = 2 * h + a
                sp.wait_ge(sums_out, u + 1)
                apart(sp, passed_sp)
                wait(sp, whole_done, u - 1)
                apart(sp, passed_sp)
                sp.dma_start(odd[a][:, :], sums[a][P // 2:P, :]).then_inc(odd_in[a], 16)

            def keep(h, a):
                sp.wait_ge(whole_done, 2 * h + a + 1)
                apart(sp, passed_sp)
                for c in range(QC):
                    at = a * HALF + c * BANK
                    sp.dma_start(t["heads"][bass.ds(h * HD, HD), at:at + BANK],
                                 whole[a][c * 32:c * 32 + HD, :]).then_inc(kept[a], 16)
                sp.dma_start(t["divisors"][bass.ds(h, 1), a * HALF:(a + 1) * HALF]
                             .rearrange("h (c n) -> (h c) n", c=QC), whole[a][HD:HD + 33:32, :]).then_inc(kept[a], 16)

            def second_stacks(h, hh):
                sp.wait_ge(first_in[hh], (h - hh + 2) * 3 * 16)
                apart(sp, passed_sp)
                wait(sp, st_done, 2 * (h - 1) * EXPS)
                for to, of in ((q2nd[hh], q1st[hh]), (k2nd[hh], k1st[hh])):
                    sp.dma_start(to[0:STACK, :], of[:, :]).then_inc(second_in[hh], 16)

            stacks(0, q1st[0], k1st[0], first_in[0])
            stacks(1, q1st[1], k1st[1], first_in[1])
            second_stacks(0, 0)
            maxima(0, 0, 0)

            def body(i, hh, first, last):
                h = 2 * i + hh
                maxima(h, hh, 1)
                if not first:
                    odd_rows(h - 1, 1)
                if not last:
                    second_stacks(h + 1, 1 - hh)
                if not first:
                    keep(h - 1, 1)
                if not last:
                    maxima(h + 1, 1 - hh, 0)
                odd_rows(h, 0)
                if not isinstance(i, int) or i < HEADS // 2 - 1:
                    sp.wait_ge(s_done, (h + 1) * 2 * MAXES)
                    sp.wait_ge(second_in[hh], (i + 1) * 2 * 16)
                    stacks(h + 2, q1st[hh], k1st[hh], first_in[hh])
                keep(h, 0)

            each_head(sp, body)
            odd_rows(HEADS - 1, 1)
            keep(HEADS - 1, 1)
            for a in range(2):
                sp.wait_ge(kept[a], HEADS * (QC + 1) * 16)

        @block.tensor
        def _(pe):
            def pass_1(h, hh, a, r):
                qt, kw = a * QT + r // KW, r % KW
                wait(pe, s_read, (2 * h + a) * MAXES + r - 1)
                for j in range(2):
                    at = kw * WIDE + j * BANK
                    mm = pe.matmul(s_ps[r % 2][:, j * BANK:(j + 1) * BANK], q1st[hh][:, qt * P:(qt + 1) * P],
                                   k1st[hh][:, at:at + BANK], start=True, stop=True)
                mm.then_inc(s_done, 1)

            def pass_2(h, hh, a, kt, c):
                e = kt * QC + c
                wait(pe, exp_done, (2 * h + a) * EXPS + before(e, ST) + 1)
                at = a * HALF + c * BANK
                pe.matmul(st_ps[e % ST][:, :], k2nd[hh][:, kt * P:(kt + 1) * P], q2nd[hh][:, at:at + BANK],
                          start=True, stop=True).then_inc(st_done, 1)

            def times_v(h, hh, a, pair):
                u = 2 * h + a
                pe.wait_ge(exp_done, u * EXPS + (pair + 1) * 2 * QC)
                if pair == 0:
                    wait(pe, sums_out, u)
                for kk in range(2):
                    for c in range(QC):
                        at = (2 * kk + c) * 32
                        mm = pe.matmul(o_ps[at:at + VM, :], v_head[hh][:, 2 * pair + kk, :],
                                       probs[pair % SLOTS][:, kk, c * BANK:(c + 1) * BANK],
                                       start=pair == 0, stop=pair == PAIRS - 1, tile_position=(0, at))
                mm.then_inc(pv_done, 1)

            pe.wait_ge(o_cleared, 1)
            pe.wait_ge(ones_set, 4)
            pe.wait_ge(first_in[0], 6 * 16)
            for a in range(2):
                for r in range(MAXES):
                    pass_1(0, 0, a, r)

            def body(i, hh, first, last):
                h = 2 * i + hh
                pe.wait_ge(second_in[hh], (i + 1) * 2 * 16)
                if not last:
                    pe.wait_ge(first_in[1 - hh], (i + hh + 1) * 6 * 16)
                for a in range(2):
                    pe.wait_ge(max_in[2 * hh + a], (i + 1) * PARTS * 16)
                    for p in range(PAIRS):
                        for kk in range(2):
                            for c in range(QC):
                                pass_2(h, hh, a, 2 * p + kk, c)
                            if not last:
                                pass_1(h + 1, 1 - hh, a, 2 * p + kk)
                        if p > 0:
                            if p == 1 and a == 0:
                                pe.wait_ge(v_ready, h + 1)
                            times_v(h, hh, a, p - 1)
                        elif a == 1:
                            times_v(h, hh, 0, PAIRS - 1)
                        elif not first:
                            times_v(h - 1, 1 - hh, 1, PAIRS - 1)

            each_head(pe, body)
            times_v(HEADS - 1, 1, 1, PAIRS - 1)

        @block.scalar
        def _(act):
            def drain(h, a):
                u = 2 * h + a
                act.wait_ge(pv_done, (u + 1) * PAIRS)
                wait(act, whole_done, u - 1)
                act.copy(sums[a][:, :], o_ps[:, :]).then_inc(sums_out, 1)

            def body(i, hh, first, last):
                h = 2 * i + hh
                for a in range(2):
                    u = 2 * h + a
                    for e in range(EXPS):
                        pair, kk, c = e // (2 * QC), e // QC % 2, e % QC
                        if e == 2 * QC and a == 1:
                            drain(h, 0)
                        elif e == 2 * QC and not first:
                            drain(h - 1, 1)
                        if e % (2 * QC) == 0:
                            wait(act, pv_done, u * PAIRS + pair - SLOTS + 1)
                        act.wait_ge(st_done, u * EXPS + e + 1)
                        act.activation(probs[pair % SLOTS][:, kk, c * BANK:(c + 1) * BANK],
                                       st_ps[e % ST][:, :], ACT.Exp, scale=SCALE).then_inc(exp_done, 1)

            each_head(act, body)
            drain(HEADS - 1, 1)

        @block.vector
        def _(dve):
            dve.memset(o_ps[:, :], 0.0).then_inc(o_cleared, 1)
            for a in range(2):
                dve.memset(neg_max[a][:, :], 0.0).then_inc(cleared, 1)
            dve.wait_ge(cleared, 2)

            def maximum(h, a, r):
                u = 2 * h + a
                if r == 0:
                    wait(dve, unit_max, u - 1)
                dve.wait_ge(s_done, u * MAXES + r + 1)
                dve.tensor_reduce(tile_max[a][:, r // KW, r % KW:r % KW + 1], s_ps[r % 2][:, :],
                                  AX.X, ALU.max).then_inc(s_read, 1)

            def unit_maxima(h, a):
                u = 2 * h + a
                dve.wait_ge(s_read, (u + 1) * MAXES)
                wait(dve, max_turned, u - 1)
                dve.tensor_reduce(neg_max[a][:, 0:QT], tile_max[a][:, :, :], AX.X, ALU.max,
                                  negate=True).then_inc(unit_max, 1)
                dve.wait_ge(unit_max, u + 1)
                wait(dve, max_cut, CUTS * (u - 1))
                dve.transpose(neg_max_t[a][:, :], neg_max[a][:, :]).then_inc(max_turned, 1)

            for a in range(2):
                for r in range(MAXES):
                    maximum(0, a, r)
                unit_maxima(0, a)

            def body(i, hh, first, last):
                h = 2 * i + hh
                for a in range(2):
                    for r in range(MAXES):
                        if not last:
                            maximum(h + 1, a, r)
                    if not last:
                        unit_maxima(h + 1, a)

            each_head(dve, body)

        @block.gpsimd
        def _(pool):
            for i in range(2):
                wait(pool, ones_set, 2 * i)
                pool.memset(k2nd[i][STACK:ROWS, :], 1.0).then_inc(ones_set, 1)
                pool.wait_ge(ones_set, 2 * i + 1)
                pool.memset(v_head[i][:, :, HD:VM], 1.0).then_inc(ones_set, 1)
            pool.wait_ge(ones_set, 4)

            def cut(h, a):
                steps = CUTS * (2 * h + a)
                pool.wait_ge(max_turned, 2 * h + a + 1)
                wait(pool, max_out[a], h * 16)
                apart(pool, passed_pool)
                pool.tensor_copy(max_parts[a][:, 0, :], neg_max_t[a][:, :]).then_inc(max_cut, 1)
                pool.wait_ge(max_cut, steps + 1)
                pool.tensor_tensor(max_rest[:, :], neg_max_t[a][:, :], max_parts[a][:, 0, :],
                                   ALU.subtract).then_inc(max_cut, 1)
                pool.wait_ge(max_cut, steps + 2)
                apart(pool, passed_pool)
                pool.tensor_copy(max_parts[a][:, 1, :], max_rest[:, :]).then_inc(max_cut, 1)
                pool.wait_ge(max_cut, steps + 3)
                pool.tensor_tensor(max_parts[a][:, 2, :], max_rest[:, :], max_parts[a][:, 1, :],
                                   ALU.subtract).then_inc(max_cut, 1)

            def head_v(h, hh):
                wait(pool, pv_done, (h - 1) * 2 * PAIRS)
                apart(pool, passed_pool)
                pool.tensor_copy(v_head[hh][:, :, 0:HD],
                                 t["kept"][:, bass.ds(h, 1), :, :].rearrange("p h k d -> p (h k) d")
                                 ).then_inc(v_ready, 1)

            def add_odd(h, a):
                pool.wait_ge(sums_out, 2 * h + a + 1)
                pool.wait_ge(odd_in[a], (h + 1) * 16)
                wait(pool, kept[a], h * (QC + 1) * 16)
                pool.tensor_tensor(whole[a][:, :], sums[a][0:P // 2, :], odd[a][:, :],
                                   ALU.add).then_inc(whole_done, 1)

            head_v(0, 0)
            cut(0, 0)

            def body(i, hh, first, last):
                h = 2 * i + hh
                cut(h, 1)
                if not first:
                    add_odd(h - 1, 1)
                if not last:
                    head_v(h + 1, 1 - hh)
                    cut(h + 1, 0)
                add_odd(h, 0)

            each_head(pool, body)
            add_odd(HEADS - 1, 1)


def finish(nc, t, B, T, D, HID):
    CH = BANK
    NCS = T // CH
    NCH = B * NCS
    TT = CH // P
    KD = D // P
    HD = D // N_HEAD
    HPT = P // HD
    HT = HID // P
    with ExitStack() as ctx:
        def sb(name, shape, dt=F32):
            return ctx.enter_context(nc.sbuf_tensor(name, shape, dt))

        def psum(name, shape):
            return ctx.enter_context(nc.psum_tensor(name, shape, F32))

        def sem(name):
            return ctx.enter_context(nc.semaphore(name))

        w_out = sb("w_out", [P, KD, D])
        b_out = sb("b_out", [P, D])
        gate_int = sb("gate_int", [P, KD, HID], I32)
        up_int = sb("up_int", [P, KD, HID], I32)
        down_int = sb("down_int", [P, HT, D], I32)
        w_gate = sb("w_gate", [P, KD, HID])
        w_up = sb("w_up", [P, KD, HID])
        w_down = sb("w_down", [P, HT, D])
        ident = sb("ident", [P, P])
        heads = [sb(f"heads{i}", [P, KD, CH]) for i in range(2)]
        x_in = [sb(f"x_in{i}", [P, TT, D]) for i in range(2)]
        inverse = [sb(f"inverse{i}", [P, KD, CH]) for i in range(2)]
        sums = [sb(f"divisors{b}", [P, N_HEAD * T // P]) for b in range(B)]
        z = sb("z", [P, TT, D])
        x1 = [sb(f"x1{i}", [P, TT, D]) for i in range(2)]
        x1_t = sb("x1_t", [P, KD, CH])
        silu = [sb(f"silu{i}", [P, CH]) for i in range(2)]
        hidden = sb("hidden", [P, HT, CH])
        y = sb("y", [P, TT, D])
        result = [sb(f"result{i}", [P, TT, D]) for i in range(2)]
        stats = sb("stats", [P, 2 * TT, 6])
        moments = sb("moments", [P, 2 * TT, 2])
        var_eps = sb("var_eps", [P, 2 * TT])
        std = sb("std", [P, 2 * TT])
        rstd = sb("rstd", [P, 2 * TT])

        t_ps = psum("t_ps", [P, KD, CH])
        p_ps = psum("p_ps", [P, TT, D])
        g_ps = [psum(f"g_ps{i}", [P, CH]) for i in range(2)]
        u_ps = [psum(f"u_ps{i}", [P, CH]) for i in range(2)]

        passed, passed_sp = sem("passed"), sem("passed_sp")
        weights_in = sem("weights_in")
        sums_in = [sem(f"sums_in{b}") for b in range(B)]
        inverted = sem("inverted")
        inverses_out = [sem(f"inverses_out{b}") for b in range(B)]
        inverse_in = [sem(f"inverse_in{i}") for i in range(2)]
        softmaxed = sem("softmaxed")
        out_bias_in = sem("out_bias_in")
        ident_set = sem("ident_set")
        dequantized = sem("dequantized")
        heads_in = [sem(f"heads_in{i}") for i in range(2)]
        x_landed = [sem(f"x_landed{i}") for i in range(2)]
        biased = sem("biased")
        proj_done = sem("proj_done")
        z_done = sem("z_done")
        z_stats = sem("z_stats")
        z_moments = sem("z_moments")
        y_stats = sem("y_stats")
        y_moments = sem("y_moments")
        var_done = sem("var_done")
        std_done = sem("std_done")
        rstd_done = sem("rstd_done")
        x1_done = sem("x1_done")
        turned = sem("turned")
        x1_t_done = sem("x1_t_done")
        gate_done = sem("gate_done")
        up_done = sem("up_done")
        silu_done = sem("silu_done")
        hidden_done = sem("hidden_done")
        down_done = sem("down_done")
        y_done = sem("y_done")
        result_done = sem("result_done")
        kept = [sem(f"kept{i}") for i in range(2)]

        def each_chunk(eng, body):
            def turn(i, first, last):
                body(2 * i, 0, first, False)
                body(2 * i + 1, 1, False, last)
            turn(0, True, False)
            with eng.Fori(1, NCH // 2 - 1) as i:
                turn(i, False, False)
            turn(NCH // 2 - 1, False, True)

        def landed(c, par):
            return (c - par + 2) * 8

        heads_dram = t["heads"].rearrange("(b g p) n -> p b g n", b=B, p=P)

        block = ctx.enter_context(nc.Block())

        @block.sync
        def _(sp):
            def load(c, par):
                wait(sp, proj_done, 2 * (c - 1))
                apart(sp, passed_sp)
                sp.dma_start(heads[par][:, :, :], heads_dram[:, bass.ds(c // NCS, 1), :, bass.ds(c % NCS * CH, CH)]
                             .rearrange("p b g n -> p (b g) n")).then_inc(heads_in[par], 16)
                for kd in range(KD):
                    row = t["inverses"][bass.ds(c // NCS * N_HEAD + kd * HPT, HPT), bass.ds(c % NCS * CH, CH)]
                    sp.dma_start(inverse[par][:, kd, :],
                                 bass.AP(tensor=row.tensor, offset=row.offset, ap=[[T, HPT], [0, HD], [1, CH]])
                                 ).then_inc(inverse_in[par], 16)
                wait(sp, z_done, 2 * (c - 1))
                apart(sp, passed_sp)
                sp.dma_start(x_in[par][:, :, :], t["x"].rearrange("(n p) d -> p n d", p=P)
                             [:, bass.ds(c * TT, TT), :]).then_inc(x_landed[par], 16)

            def spread_out(what, b):
                return t[what][b * N_HEAD:(b + 1) * N_HEAD, :].rearrange("h (q n) -> (h q) n", q=P // N_HEAD)

            for b in range(B):
                sp.dma_start(sums[b][:, :], spread_out("divisors", b)).then_inc(sums_in[b], 16)
            sp.dma_start(w_out[:, :, :], t["w_out"].rearrange("(k p) n -> p k n", p=P)).then_inc(weights_in, 16)
            for b in range(B):
                sp.wait_ge(inverted, b + 1)
                sp.dma_start(spread_out("inverses", b), sums[b][:, :]).then_inc(inverses_out[b], 16)
            for b in range(B):
                sp.wait_ge(inverses_out[b], 16)
            load(0, 0)
            for to, name in ((gate_int, "w_gate_t"), (up_int, "w_up_t"), (down_int, "w_down_t")):
                sp.dma_start(to[:, :, :], t[name].rearrange("(k p) n -> p k n", p=P)).then_inc(weights_in, 16)
            load(1, 1)

            def body(c, par, first, last):
                if not isinstance(c, int) or c + 2 < NCH:
                    load(c + 2, par)
                if not first:
                    keep(c - 1, 1 - par)

            def keep(c, par):
                sp.wait_ge(result_done, c + 1)
                sp.dma_start(t["out"].rearrange("(n p) d -> p n d", p=P)[:, bass.ds(c * TT, TT), :],
                             result[par][:, :, :]).then_inc(kept[par], 16)

            each_chunk(sp, body)
            keep(NCH - 1, 1)
            for par in range(2):
                sp.wait_ge(kept[par], NCH // 2 * 16)

        @block.tensor
        def _(pe):
            def output_projection(c, par):
                pe.wait_ge(softmaxed, c + 1)
                wait(pe, y_done, 2 * (c - 1))
                for n in range(TT):
                    for kd in range(KD):
                        mm = pe.matmul(p_ps[:, n, :], heads[par][:, kd, n * P:(n + 1) * P], w_out[:, kd, :],
                                       start=kd == 0, stop=kd == KD - 1)
                    if n % 2 == 1:
                        mm.then_inc(proj_done, 1)

            pe.wait_ge(weights_in, 4 * 16)
            pe.wait_ge(ident_set, 2)
            pe.wait_ge(dequantized, 3)
            output_projection(0, 0)

            def body(c, par, first, last):
                pe.wait_ge(x1_done, c + 1)
                wait(pe, x1_t_done, KD * c)
                for kd in range(KD):
                    for n in range(TT):
                        mm = pe.transpose(t_ps[:, kd, n * P:(n + 1) * P], x1[par][:, n, kd * P:(kd + 1) * P],
                                          ident[:, :])
                    mm.then_inc(turned, 1)
                if not last:
                    output_projection(c + 1, 1 - par)
                pe.wait_ge(x1_t_done, KD * (c + 1))
                for m in range(HT):
                    wait(pe, silu_done, c * HT + m - 1)
                    for kd in range(KD):
                        mm = pe.matmul(g_ps[m % 2][:, :], w_gate[:, kd, m * P:(m + 1) * P], x1_t[:, kd, :],
                                       start=kd == 0, stop=kd == KD - 1)
                    mm.then_inc(gate_done, 1)
                    wait(pe, hidden_done, c * HT + m - 1)
                    for kd in range(KD):
                        mm = pe.matmul(u_ps[m % 2][:, :], w_up[:, kd, m * P:(m + 1) * P], x1_t[:, kd, :],
                                       start=kd == 0, stop=kd == KD - 1)
                    mm.then_inc(up_done, 1)
                pe.wait_ge(hidden_done, (c + 1) * HT)
                if not last:
                    pe.wait_ge(z_done, 2 * (c + 2))
                for n in range(TT):
                    for m in range(HT):
                        mm = pe.matmul(p_ps[:, n, :], hidden[:, m, n * P:(n + 1) * P], w_down[:, m, :],
                                       start=m == 0, stop=m == HT - 1)
                    if n % 2 == 1:
                        mm.then_inc(down_done, 1)

            each_chunk(pe, body)

        @block.scalar
        def _(act):
            def deviations(k):
                act.wait_ge(var_done, k + 1)
                wait(act, rstd_done, k)
                act.activation(std[:, :], var_eps[:, :], ACT.Sqrt).then_inc(std_done, 1)

            deviations(0)

            def body(c, par, first, last):
                for kd in range(KD):
                    act.wait_ge(turned, KD * c + kd + 1)
                    act.copy(x1_t[:, kd, :], t_ps[:, kd, :]).then_inc(x1_t_done, 1)
                for m in range(HT):
                    act.wait_ge(gate_done, c * HT + m + 1)
                    wait(act, hidden_done, c * HT + m - 1)
                    act.activation(silu[m % 2][:, :], g_ps[m % 2][:, :], ACT.Silu).then_inc(silu_done, 1)
                    if m == 1:
                        deviations(c + 1)

            each_chunk(act, body)
            deviations(NCH + 1)

        @block.vector
        def _(dve):
            for b in range(B):
                dve.wait_ge(sums_in[b], 16)
                dve.reciprocal(sums[b][:, :], sums[b][:, :]).then_inc(inverted, 1)
            for to, of, n in ((w_gate, gate_int, 1), (w_up, up_int, 2), (w_down, down_int, 3)):
                if n == 1:
                    dve.wait_ge(weights_in, 4 * 16)
                dve.tensor_scalar(to[:, :, :], of[:, :, :], float(np.float32(QUANT_SCALE)), None,
                                  ALU.mult).then_inc(dequantized, 1)
            dve.memset(moments[:, :, :], 1.0).then_inc(z_moments, 1)
            dve.wait_ge(z_moments, 1)

            def statistics(src, at, n0, counted, averaged):
                for n in range(TT):
                    dve.bn_stats(stats[:, at + n, :], src[:, n, :]).then_inc(counted, 1)
                dve.wait_ge(counted, TT * (n0 + 1))
                apart(dve, passed)
                for n in range(TT):
                    dve.bn_aggr(moments[:, at + n, :], stats[:, at + n, :]).then_inc(averaged, 1)

            def sum_z(c, par):
                dve.wait_ge(biased, c + 1)
                for j in range(2):
                    dve.wait_ge(proj_done, 2 * c + j + 1)
                    if j == 0:
                        wait(dve, x1_done, c)
                    dve.tensor_tensor(z[:, 2 * j:2 * j + 2, :], p_ps[:, 2 * j:2 * j + 2, :],
                                      x_in[par][:, 2 * j:2 * j + 2, :], ALU.add).then_inc(z_done, 1)
                dve.wait_ge(z_done, 2 * c + 2)
                wait(dve, z_moments, 1 + TT * c)
                wait(dve, var_done, c)
                statistics(z, 0, c, z_stats, z_moments)

            def sum_y(c, par):
                for j in range(2):
                    dve.wait_ge(down_done, 2 * c + j + 1)
                    if j == 0:
                        wait(dve, result_done, c)
                    dve.tensor_tensor(y[:, 2 * j:2 * j + 2, :], p_ps[:, 2 * j:2 * j + 2, :],
                                      x1[par][:, 2 * j:2 * j + 2, :], ALU.add).then_inc(y_done, 1)
                dve.wait_ge(y_done, 2 * c + 2)
                wait(dve, y_moments, TT * c)
                wait(dve, var_done, c + 2)
                statistics(y, TT, c, y_stats, y_moments)

            def variances(k, zs, ys):
                dve.wait_ge(z_moments, 1 + TT * zs)
                wait(dve, y_moments, TT * ys)
                wait(dve, std_done, k)
                dve.tensor_scalar(var_eps[:, :], moments[:, :, 1], EPS, None, ALU.add).then_inc(var_done, 1)

            def invert(k, x1s, results):
                dve.wait_ge(std_done, k + 1)
                wait(dve, x1_done, x1s)
                wait(dve, result_done, results)
                dve.reciprocal(rstd[:, :], std[:, :]).then_inc(rstd_done, 1)
                dve.wait_ge(rstd_done, k + 1)

            def normalize(to, of, at, done):
                for n in range(TT):
                    last = dve.tensor_scalar(to[:, n, :], of[:, n, :], moments[:, at + n, 0:1],
                                             rstd[:, at + n:at + n + 1], ALU.subtract, ALU.mult)
                last.then_inc(done, 1)

            def hide(c, m):
                dve.wait_ge(silu_done, c * HT + m + 1)
                dve.wait_ge(up_done, c * HT + m + 1)
                dve.tensor_tensor(hidden[:, m, :], u_ps[m % 2][:, :], silu[m % 2][:, :],
                                  ALU.mult).then_inc(hidden_done, 1)

            sum_z(0, 0)
            variances(0, 1, 0)
            invert(0, 0, 0)
            normalize(x1[0], z, 0, x1_done)

            def body(c, par, first, last):
                if not first:
                    sum_y(c - 1, 1 - par)
                if not last:
                    sum_z(c + 1, 1 - par)
                variances(c + 1, NCH if last else c + 2, c)
                hide(c, 0)
                hide(c, 1)
                invert(c + 1, c + 1, c - 1)
                if not last:
                    normalize(x1[1 - par], z, 0, x1_done)
                if not first:
                    wait(dve, kept[1 - par], landed(c - 1, 1 - par) - 16)
                    normalize(result[1 - par], y, TT, result_done)
                for m in range(2, HT):
                    hide(c, m)

            each_chunk(dve, body)
            sum_y(NCH - 1, 1)
            variances(NCH + 1, NCH, NCH)
            invert(NCH + 1, NCH, NCH - 1)
            dve.wait_ge(kept[1], landed(NCH - 1, 1) - 16)
            normalize(result[1], y, TT, result_done)

        @block.gpsimd
        def _(pool):
            pool.dma_start(b_out[:, :], bass.AP(tensor=t["b_out"].tensor, offset=0,
                                                ap=[[0, P], [1, D]])).then_inc(out_bias_in, 16)
            pool.memset(ident[:, :], 0.0).then_inc(ident_set, 1)
            pool.wait_ge(ident_set, 1)
            pool.affine_select(out=ident[:, :], in_=ident[:, :], compare_op=ALU.not_equal, fill=1.0, base=0,
                               pattern=[[-1, P]], channel_multiplier=1).then_inc(ident_set, 1)
            pool.wait_ge(out_bias_in, 16)

            def divide(c, par):
                pool.wait_ge(heads_in[par], landed(c, par))
                pool.wait_ge(inverse_in[par], KD * landed(c, par))
                pool.tensor_tensor(heads[par][:, :, :], heads[par][:, :, :], inverse[par][:, :, :],
                                   ALU.mult).then_inc(softmaxed, 1)

            def bias(c, par):
                pool.wait_ge(x_landed[par], landed(c, par))
                pool.tensor_tensor(x_in[par][:, :, :], x_in[par][:, :, :],
                                   b_out[:, :].unsqueeze(1).broadcast_to([P, TT, D]), ALU.add).then_inc(biased, 1)

            divide(0, 0)
            bias(0, 0)

            def body(c, par, first, last):
                if not last:
                    divide(c + 1, 1 - par)
                    bias(c + 1, 1 - par)

            each_chunk(pool, body)


def layer(nc, t, B, T, D, HID):
    HD = D // N_HEAD
    HEADS = B * N_HEAD
    t["q_parts"] = nc.dram_tensor("q_parts", [HEADS, HD, PARTS, T], BF16).ap()
    t["k_parts"] = nc.dram_tensor("k_parts", [HEADS, HD, PARTS, T], BF16).ap()
    t["max_parts"] = nc.dram_tensor("max_parts_out", [4, P, PARTS, 32], BF16).ap()
    t["heads"] = nc.dram_tensor("heads_out", [HEADS * HD, T], F32).ap()
    t["divisors"] = nc.dram_tensor("divisors_out", [HEADS, T], F32).ap()
    t["inverses"] = nc.dram_tensor("inverses_out", [HEADS, T], F32).ap()
    with nc.sbuf_tensor("kept_v", [P, HEADS, T // P, HD], F32) as kept:
        t["kept"] = kept
        project(nc, t, B, T, D)
        attend(nc, t, B, T, D)
    finish(nc, t, B, T, D, HID)


def rotary_tables(T, hd, rows):
    inv = (np.float32(1.0) / np.float32(10000.0) ** (np.arange(0, hd, 2, dtype=np.float32) / np.float32(hd)))
    angle = np.repeat(np.arange(T, dtype=np.float32)[:, None] * inv.astype(np.float32)[None, :], 2, axis=1).T
    sign = np.where(np.arange(hd) % 2 == 0, -1.0, 1.0).astype(np.float32)[:, None]
    return (np.ascontiguousarray(np.tile(np.cos(angle), (rows // hd, 1)), np.float32),
            np.ascontiguousarray(np.tile(np.sin(angle) * sign, (rows // hd, 1)), np.float32))


def kernel(L0_attn_x, L0_attn_w_qkv, L0_attn_b_qkv, L0_attn_w_out, L0_attn_b_out,
           L0_ffn_w_gate, L0_ffn_w_up, L0_ffn_w_down):
    import concourse.bacc as bacc
    from concourse.bass_utils import run_bass_kernel_spmd

    x = np.asarray(L0_attn_x)
    B, T, D = x.shape
    HID = L0_ffn_w_gate.shape[0]
    cos, sin = rotary_tables(T, D // N_HEAD, P)
    flat = x.reshape(B * T, D)
    arrays = {
        "x": np.ascontiguousarray(flat),
        "x_t": np.ascontiguousarray(flat.T),
        "w_qkv": np.ascontiguousarray(L0_attn_w_qkv),
        "b_qkv": np.ascontiguousarray(L0_attn_b_qkv),
        "b_qkv_cols": np.ascontiguousarray(np.asarray(L0_attn_b_qkv).reshape(3 * D // P, P).T),
        "w_out": np.ascontiguousarray(L0_attn_w_out),
        "b_out": np.ascontiguousarray(L0_attn_b_out),
        "w_gate_t": np.ascontiguousarray(np.asarray(L0_ffn_w_gate).T),
        "w_up_t": np.ascontiguousarray(np.asarray(L0_ffn_w_up).T),
        "w_down_t": np.ascontiguousarray(np.asarray(L0_ffn_w_down).T),
        "cos": cos,
        "sin": sin,
    }
    nc = bacc.Bacc("TRN2", target_bir_lowering=False, num_devices=1)
    t = {n: nc.dram_tensor("in_" + n, a.shape, mybir.dt.from_np(a.dtype), kind="ExternalInput").ap()
         for n, a in arrays.items()}
    t["out"] = nc.dram_tensor("out", (B * T, D), F32, kind="ExternalOutput").ap()
    layer(nc, t, B, T, D, HID)
    r = run_bass_kernel_spmd(nc, [{"in_" + n: a for n, a in arrays.items()}], core_ids=[0])
    return r.results[0]["out"].reshape(B, T, D)
```

```python
from contextlib import ExitStack

import numpy as np

import concourse.bass as bass
from concourse import mybir

P = 128
N_HEAD = 16
FFN = ("w_gate", "w_up", "w_down")
PARTS = 3
BANK = 512
EPS = 1e-5
QUANT_SCALE = float(np.float32(1.0 / 127.0))
NARROW = 127
X1_SCALE = 2.0 ** 11
HIDDEN_SCALE = 2.0 ** -1
WIDE_SCALE = 2.0 ** -49

F32 = mybir.dt.float32
BF16 = mybir.dt.bfloat16
F16 = mybir.dt.float16
I32 = mybir.dt.int32
ACT = mybir.ActivationFunctionType
ALU = mybir.AluOpType
AX = mybir.AxisListType


def wait(eng, sem, value):
    if not isinstance(value, int) or value > 0:
        eng.wait_ge(sem, value)


def apart(eng, passed):
    eng.sem_inc(passed, 1)


def project(nc, t, B, T, D):
    CH = BANK
    NC = T // CH
    KD = D // P
    M = 2 * KD
    HPT = P // (D // N_HEAD)
    HD = D // N_HEAD
    swap = [p ^ 1 for p in range(32)]
    with ExitStack() as ctx:
        def sb(name, shape, dt):
            return ctx.enter_context(nc.sbuf_tensor(name, shape, dt))

        def sem(name):
            return ctx.enter_context(nc.semaphore(name))

        w_qkv = sb("w_qkv", [P, KD, 3 * D], F32)
        bias_qk = sb("bias_qk", [P, 3 * KD], F32)
        bias_v = sb("bias_v", [P, D], F32)
        cos = sb("cos", [P, T], F32)
        sin = sb("sin", [P, T], F32)
        x_t = [sb(f"x_t{i}", [P, KD, CH], F32) for i in range(2)]
        raw = [sb(f"raw{i}", [P, M, CH], F32) for i in range(2)]
        turned = [sb(f"turned{i}", [P, M, CH], F32) for i in range(2)]
        roped = [sb(f"roped{i}", [P, M, CH], F32) for i in range(2)]
        rest = [sb(f"rest{i}", [P, M, CH], F32) for i in range(2)]
        parts = [sb(f"parts{i}", [P, M, PARTS, CH], BF16) for i in range(2)]
        qk_ps = [ctx.enter_context(nc.psum_tensor(f"qk_ps{m}", [P, CH], F32)) for m in range(M)]
        v_ps = [ctx.enter_context(nc.psum_tensor(f"v_ps{n}", [P, 2, D], F32)) for n in range(2)]

        passed = sem("passed")
        weights_in = sem("weights_in")
        bias_in = sem("bias_in")
        tables_in = sem("tables_in")
        x_in = [sem(f"x_in{i}") for i in range(2)]
        qk_done = sem("qk_done")
        v_done = sem("v_done")
        raw_done = sem("raw_done")
        v_kept = sem("v_kept")
        swapped = sem("swapped")
        cosined = sem("cosined")
        sined = sem("sined")
        roped_done = sem("roped_done")
        part1_done = sem("part1_done")
        rest1_done = sem("rest1_done")
        part2_done = sem("part2_done")
        part3_done = sem("part3_done")
        stored = [sem(f"stored{i}") for i in range(2)]

        block = ctx.enter_context(nc.Block())

        def each_sequence(eng, body):
            def turn(b, first, last):
                for c in range(NC):
                    body(b, c, first and c == 0, last and c == NC - 1)
            turn(0, True, False)
            if B > 2:
                with eng.Fori(1, B - 1) as b:
                    turn(b, False, False)
            turn(B - 1, False, True)

        @block.sync
        def _(sp):
            def body(b, c, first, last):
                k = b * NC + c
                wait(sp, v_done, (k - 1) * 2)
                sp.dma_start(x_t[c % 2][:, :, :],
                             t["x_t"].rearrange("(k p) n -> p k n", p=P)[:, :, bass.ds(k * CH, CH)]
                             ).then_inc(x_in[c % 2], 16)
                if first:
                    sp.dma_start(sin[:, :], t["sin"]).then_inc(tables_in, 16)
                    sp.dma_start(cos[:, :], t["cos"]).then_inc(tables_in, 16)
                    sp.dma_start(bias_v[:, :], bass.AP(tensor=t["b_qkv"].tensor, offset=2 * D,
                                                       ap=[[0, P], [1, D]])).then_inc(tables_in, 16)

            sp.dma_start(w_qkv[:, :, :], t["w_qkv"].rearrange("(k p) n -> p k n", p=P)).then_inc(weights_in, 16)
            each_sequence(sp, body)

        @block.tensor
        def _(pe):
            def body(b, c, first, last):
                k = b * NC + c
                x = x_t[c % 2]
                pe.wait_ge(x_in[c % 2], (b * (NC // 2) + c // 2 + 1) * 16)
                for m in range(M):
                    wait(pe, raw_done, (k - 1) * M + m + 1)
                    for kd in range(KD):
                        mm = pe.matmul(qk_ps[m][:, :], w_qkv[:, kd, m * P:(m + 1) * P], x[:, kd, :],
                                       start=kd == 0, stop=kd == KD - 1)
                    mm.then_inc(qk_done, 1)
                for n in range(2):
                    wait(pe, v_kept, (k - 1) * 2 + n + 1)
                    for j in range(2):
                        at = (2 * n + j) * P
                        for kd in range(KD):
                            mm = pe.matmul(v_ps[n][:, j, :], x[:, kd, at:at + P], w_qkv[:, kd, 2 * D:3 * D],
                                           start=kd == 0, stop=kd == KD - 1)
                    mm.then_inc(v_done, 1)

            pe.wait_ge(weights_in, 16)
            each_sequence(pe, body)


        @block.scalar
        def _(act):
            def evacuate(k, i):
                for m in range(M):
                    act.wait_ge(qk_done, k * M + m + 1)
                    if m == 0:
                        wait(act, cosined, k - 1)
                    act.activation(raw[i][:, m, :], qk_ps[m][:, :], ACT.Identity,
                                   bias=bias_qk[:, m:m + 1]).then_inc(raw_done, 1)

            def part_1(k, i):
                act.wait_ge(roped_done, k + 1)
                wait(act, stored[i], (k - i) * 8 * M)
                act.activation(parts[i][:, :, 0, :], roped[i][:, :, :], ACT.Copy).then_inc(part1_done, 1)

            def part_2(k, i):
                act.wait_ge(rest1_done, k + 1)
                act.activation(parts[i][:, :, 1, :], rest[i][:, :, :], ACT.Copy).then_inc(part2_done, 1)

            def store(b, c):
                act.wait_ge(part3_done, b * NC + c + 1)
                for m in range(M):
                    to = t["q_parts"] if m < KD else t["k_parts"]
                    row = (b * N_HEAD + (m % KD) * HPT) * HD
                    to = to.rearrange("h d a n -> (h d) a n")
                    act.dma_start(to[bass.ds(row, P), :, c * CH:(c + 1) * CH],
                                  parts[c % 2][:, m, :, :]).then_inc(stored[c % 2], 16)

            def body(b, c, first, last):
                k = b * NC + c
                i = c % 2
                if not first:
                    part_1(k - 1, 1 - i)
                if not last:
                    evacuate(k + 1, 1 - i)
                if not first:
                    part_2(k - 1, 1 - i)
                if c >= 2:
                    store(b, c - 2)
                elif not isinstance(b, int) or b > 0:
                    store(b - 1, NC + c - 2)

            act.dma_start(bias_qk[:, :], t["b_qkv_cols"]).then_inc(bias_in, 16)
            act.wait_ge(bias_in, 16)
            evacuate(0, 0)
            each_sequence(act, body)
            part_1(B * NC - 1, 1)
            part_2(B * NC - 1, 1)
            store(B - 1, NC - 2)
            store(B - 1, NC - 1)
            for i in range(2):
                act.wait_ge(stored[i], B * (NC // 2) * 16 * M)

        @block.vector
        def _(dve):
            def rest_1(k, i):
                dve.wait_ge(part1_done, k + 1)
                wait(dve, part3_done, k - 1)
                dve.tensor_tensor(rest[i][:, :, :], roped[i][:, :, :], parts[i][:, :, 0, :],
                                  ALU.subtract).then_inc(rest1_done, 1)

            def body(b, c, first, last):
                k = b * NC + c
                i = c % 2
                for m in range(M):
                    dve.wait_ge(raw_done, k * M + m + 1)
                    if m == 0:
                        wait(dve, roped_done, k - 1)
                    apart(dve, passed)
                    last = dve.stream_shuffle(turned[i][:, m, :], raw[i][:, m, :], swap)
                last.then_inc(swapped, 1)
                wait(dve, rest1_done, k - 1)
                wait(dve, part1_done, k - 1)
                if first:
                    dve.wait_ge(tables_in, 3 * 16)
                dve.tensor_tensor(roped[i][:, :, :], raw[i][:, :, :],
                                  cos[:, c * CH:(c + 1) * CH].unsqueeze(1).broadcast_to([P, M, CH]),
                                  ALU.mult).then_inc(cosined, 1)
                for n in range(2):
                    dve.wait_ge(v_done, k * 2 + n + 1)
                    kt = c * (CH // P) + 2 * n
                    dve.tensor_tensor(
                        t["kept"][:, bass.ds(b * N_HEAD, N_HEAD), kt:kt + 2, :].rearrange("p h k d -> p k h d"),
                        v_ps[n][:, :, :].rearrange("p k (h d) -> p k h d", d=HD),
                        bias_v[:, :].rearrange("p (h d) -> p h d", d=HD).unsqueeze(1)
                        .broadcast_to([P, 2, N_HEAD, HD]), ALU.add).then_inc(v_kept, 1)
                if not first:
                    rest_1(k - 1, 1 - i)
                dve.wait_ge(cosined, k + 1)
                dve.wait_ge(sined, k + 1)
                dve.tensor_tensor(roped[i][:, :, :], roped[i][:, :, :], turned[i][:, :, :],
                                  ALU.add).then_inc(roped_done, 1)

            each_sequence(dve, body)
            rest_1(B * NC - 1, 1)

        @block.gpsimd
        def _(pool):
            def part_3(k, i):
                pool.wait_ge(part2_done, k + 1)
                pool.tensor_tensor(parts[i][:, :, 2, :], rest[i][:, :, :], parts[i][:, :, 1, :],
                                   ALU.subtract).then_inc(part3_done, 1)

            def body(b, c, first, last):
                k = b * NC + c
                i = c % 2
                pool.wait_ge(swapped, k + 1)
                pool.tensor_tensor(turned[i][:, :, :], turned[i][:, :, :],
                                   sin[:, c * CH:(c + 1) * CH].unsqueeze(1).broadcast_to([P, M, CH]),
                                   ALU.mult).then_inc(sined, 1)
                if not first:
                    part_3(k - 1, 1 - i)

            pool.wait_ge(tables_in, 3 * 16)
            each_sequence(pool, body)
            part_3(B * NC - 1, 1)


def attend(nc, t, w, B, T, D):
    HD = D // N_HEAD
    HEADS = B * N_HEAD
    HALF = T // 2
    KT = T // P
    PAIRS = KT // 2
    QC = HALF // BANK
    QT = HALF // P
    EXPS = KT * QC
    WIDE = 2 * BANK
    KW = T // WIDE
    MAXES = QT * KW
    ST = 3
    SLOTS = 4
    STACK = 6 * HD
    ROWS = STACK + PARTS
    CUTS = 4
    VM = HD + 1
    SCALE = float(HD) ** -0.5
    assert QC == 2 and KW * QT == KT and MAXES == KT
    with ExitStack() as ctx:
        def sb(name, shape, dt):
            return ctx.enter_context(nc.sbuf_tensor(name, shape, dt))

        def psum(name, shape):
            return ctx.enter_context(nc.psum_tensor(name, shape, F32))

        def sem(name):
            return ctx.enter_context(nc.semaphore(name))

        q1st = [sb(f"q1st{i}", [STACK, T], BF16) for i in range(2)]
        k1st = [sb(f"k1st{i}", [STACK, T], BF16) for i in range(2)]
        q2nd = [sb(f"q2nd{i}", [ROWS, T], BF16) for i in range(2)]
        k2nd = [sb(f"k2nd{i}", [ROWS, T], BF16) for i in range(2)]
        v_head = [sb(f"v_head{i}", [P, KT, VM], F32) for i in range(2)]
        probs = [sb(f"probs{i}", [P, 2, HALF], F32) for i in range(SLOTS)]
        tile_max = [sb(f"tile_max{i}", [P, QT, KW], F32) for i in range(2)]
        neg_max = [sb(f"neg_max{i}", [P, 32], F32) for i in range(2)]
        neg_max_t = [sb(f"neg_max_t{i}", [P, 32], F32) for i in range(2)]
        max_parts = [sb(f"max_parts{i}", [P, PARTS, 32], BF16) for i in range(2)]
        max_rest = sb("max_rest", [P, 32], F32)
        sums = [sb(f"sums{i}", [P, BANK], F32) for i in range(2)]
        odd = [sb(f"odd{i}", [P // 2, BANK], F32) for i in range(2)]
        whole = [sb(f"whole{i}", [P // 2, BANK], F32) for i in range(2)]

        spread = [sb(f"spread{i}", [P, HALF // P], F32) for i in range(2)]

        st_ps = [psum(f"st_ps{i}", [P, BANK]) for i in range(ST)]
        s_ps = [psum(f"s_ps{i}", [P, WIDE]) for i in range(2)]
        o_ps = psum("o_ps", [P, BANK])

        passed_sp, passed_pool = sem("passed_sp"), sem("passed_pool")
        ones_set = sem("ones_set")
        o_cleared = sem("o_cleared")
        first_in = [sem(f"first_in{i}") for i in range(2)]
        second_in = [sem(f"second_in{i}") for i in range(2)]
        max_in = [sem(f"max_in{i}") for i in range(4)]
        max_out = [sem(f"max_out{i}") for i in range(2)]
        v_ready = sem("v_ready")
        s_done = sem("s_done")
        s_read = sem("s_read")
        unit_max = sem("unit_max")
        max_turned = sem("max_turned")
        max_cut = sem("max_cut")
        cleared = sem("cleared")
        st_done = sem("st_done")
        exp_done = sem("exp_done")
        pv_done = sem("pv_done")
        sums_out = sem("sums_out")
        odd_in = [sem(f"odd_in{i}") for i in range(2)]
        whole_done = sem("whole_done")
        kept = [sem(f"kept{i}") for i in range(2)]
        spread_in = [sem(f"spread_in{i}") for i in range(2)]
        inverted = sem("inverted")
        inverses_out = [sem(f"inverses_out{i}") for i in range(2)]

        def each_head(eng, body):
            def turn(i, first, last):
                body(i, 0, first, False)
                body(i, 1, False, last)
            turn(0, True, False)
            with eng.Fori(1, HEADS // 2 - 1) as i:
                turn(i, False, False)
            turn(HEADS // 2 - 1, False, True)

        def before(e, ring):
            return e - ring if e >= ring else max(j for j in range(EXPS) if j % ring == e) - EXPS

        ints = [sb(f"{name}_int", list(w[name].shape), I32) for name in FFN]
        tops = sb("tops", [P, 2 * len(FFN)], F32)
        top = sb("top", [P, 1], F32)
        ffn_in = sem("ffn_in")
        out_in = sem("out_in")
        floats = sem("floats")
        topped = sem("topped")
        ident_set = sem("ident_set")

        block = ctx.enter_context(nc.Block())

        @block.sync
        def _(sp):
            def stacks(h, q_to, k_to, landed):
                def rows(parts, part, n, step):
                    head = parts[bass.ds(h, 1), :, :, :]
                    return bass.AP(tensor=head.tensor, offset=head.offset + part * T,
                                   ap=[[step, n], [PARTS * T, HD], [1, T]])
                at = 0
                for part, n in ((0, 3), (1, 2), (2, 1)):
                    sp.dma_start(q_to[at:at + n * HD, :], rows(t["q_parts"], part, n, 0)).then_inc(landed, 16)
                    at += n * HD
                at = 0
                for n in (3, 2, 1):
                    sp.dma_start(k_to[at:at + n * HD, :], rows(t["k_parts"], 0, n, T)).then_inc(landed, 16)
                    at += n * HD

            def maxima(h, hh, a):
                sp.wait_ge(max_cut, CUTS * (2 * h + a + 1))
                apart(sp, passed_sp)
                wait(sp, st_done, (2 * (h - 2) + a + 1) * EXPS)
                four = 2 * hh + a
                there = t["max_parts"][four]
                sp.dma_start(there, max_parts[a][:, :, :]).then_inc(max_out[a], 16)
                sp.wait_ge(max_out[a], (h + 1) * 16)
                for part in range(PARTS):
                    rows = bass.AP(tensor=there.tensor, offset=there.offset + part * 32,
                                   ap=[[PARTS * 32, QT], [32 * PARTS * 32, P // 32], [1, 32]])
                    sp.dma_start(q2nd[hh][STACK + part:STACK + part + 1, a * HALF:(a + 1) * HALF], rows
                                 ).then_inc(max_in[four], 16)

            def odd_rows(h, a):
                u = 2 * h + a
                sp.wait_ge(sums_out, u + 1)
                apart(sp, passed_sp)
                wait(sp, whole_done, u - 1)
                apart(sp, passed_sp)
                sp.dma_start(odd[a][:, :], sums[a][P // 2:P, :]).then_inc(odd_in[a], 16)

            def keep(h, a):
                sp.wait_ge(whole_done, 2 * h + a + 1)
                apart(sp, passed_sp)
                for c in range(QC):
                    at = a * HALF + c * BANK
                    sp.dma_start(t["heads"][bass.ds(h * HD, HD), at:at + BANK],
                                 whole[a][c * 32:c * 32 + HD, :]).then_inc(kept[a], 16)
                wait(sp, inverses_out[a], h * 16)
                apart(sp, passed_sp)
                for c in range(QC):
                    sp.dma_start(spread[a][c * P // QC:(c + 1) * P // QC, :],
                                 whole[a][c * 32 + HD:c * 32 + HD + 1, :].rearrange("o (p n) -> o p n", p=P // QC)
                                 ).then_inc(spread_in[a], 16)

            def inverses(h, a):
                sp.wait_ge(inverted, 2 * h + a + 1)
                apart(sp, passed_sp)
                sp.dma_start(t["inverses"][bass.ds(h, 1), a * HALF:(a + 1) * HALF]
                             .rearrange("h (p n) -> (h p) n", p=P), spread[a][:, :]).then_inc(inverses_out[a], 16)

            def second_stacks(h, hh):
                sp.wait_ge(first_in[hh], (h - hh + 2) * 3 * 16)
                apart(sp, passed_sp)
                wait(sp, st_done, 2 * (h - 1) * EXPS)
                for to, of in ((q2nd[hh], q1st[hh]), (k2nd[hh], k1st[hh])):
                    sp.dma_start(to[0:STACK, :], of[:, :]).then_inc(second_in[hh], 16)

            stacks(0, q1st[0], k1st[0], first_in[0])
            stacks(1, q1st[1], k1st[1], first_in[1])
            second_stacks(0, 0)
            for name, to in zip(FFN, ints):
                sp.dma_start(to[:, :, :], t[name].rearrange("(k p) n -> p k n", p=P)).then_inc(ffn_in, 16)
            sp.dma_start(w["w_out"][:, :, :], t["w_out"].rearrange("(k p) n -> p k n", p=P)).then_inc(out_in, 16)
            sp.dma_start(w["b_out"][:, :], bass.AP(tensor=t["b_out"].tensor, offset=0,
                                                   ap=[[0, P], [1, D]])).then_inc(out_in, 16)
            maxima(0, 0, 0)

            def body(i, hh, first, last):
                h = 2 * i + hh
                maxima(h, hh, 1)
                if not first:
                    inverses(h - 1, 0)
                    odd_rows(h - 1, 1)
                if not last:
                    second_stacks(h + 1, 1 - hh)
                if not first:
                    keep(h - 1, 1)
                if not last:
                    maxima(h + 1, 1 - hh, 0)
                if not first:
                    inverses(h - 1, 1)
                odd_rows(h, 0)
                if not isinstance(i, int) or i < HEADS // 2 - 1:
                    sp.wait_ge(s_done, (h + 1) * 2 * MAXES)
                    sp.wait_ge(second_in[hh], (i + 1) * 2 * 16)
                    stacks(h + 2, q1st[hh], k1st[hh], first_in[hh])
                keep(h, 0)

            each_head(sp, body)
            odd_rows(HEADS - 1, 1)
            inverses(HEADS - 1, 0)
            keep(HEADS - 1, 1)
            inverses(HEADS - 1, 1)
            sp.wait_ge(out_in, 2 * 16)
            for a in range(2):
                sp.wait_ge(kept[a], HEADS * QC * 16)
                sp.wait_ge(inverses_out[a], HEADS * 16)

        @block.tensor
        def _(pe):
            def pass_1(h, hh, a, r):
                qt, kw = a * QT + r // KW, r % KW
                wait(pe, s_read, (2 * h + a) * MAXES + r - 1)
                for j in range(2):
                    at = kw * WIDE + j * BANK
                    mm = pe.matmul(s_ps[r % 2][:, j * BANK:(j + 1) * BANK], q1st[hh][:, qt * P:(qt + 1) * P],
                                   k1st[hh][:, at:at + BANK], start=True, stop=True)
                mm.then_inc(s_done, 1)

            def pass_2(h, hh, a, kt, c):
                e = kt * QC + c
                wait(pe, exp_done, (2 * h + a) * EXPS + before(e, ST) + 1)
                at = a * HALF + c * BANK
                pe.matmul(st_ps[e % ST][:, :], k2nd[hh][:, kt * P:(kt + 1) * P], q2nd[hh][:, at:at + BANK],
                          start=True, stop=True).then_inc(st_done, 1)

            def times_v(h, hh, a, pair):
                u = 2 * h + a
                pe.wait_ge(exp_done, u * EXPS + (pair + 1) * 2 * QC)
                if pair == 0:
                    wait(pe, sums_out, u)
                for kk in range(2):
                    for c in range(QC):
                        at = (2 * kk + c) * 32
                        mm = pe.matmul(o_ps[at:at + VM, :], v_head[hh][:, 2 * pair + kk, :],
                                       probs[pair % SLOTS][:, kk, c * BANK:(c + 1) * BANK],
                                       start=pair == 0, stop=pair == PAIRS - 1, tile_position=(0, at))
                mm.then_inc(pv_done, 1)

            pe.wait_ge(o_cleared, 1)
            pe.wait_ge(ones_set, 4)
            pe.wait_ge(first_in[0], 6 * 16)
            for a in range(2):
                for r in range(MAXES):
                    pass_1(0, 0, a, r)

            def body(i, hh, first, last):
                h = 2 * i + hh
                pe.wait_ge(second_in[hh], (i + 1) * 2 * 16)
                if not last:
                    pe.wait_ge(first_in[1 - hh], (i + hh + 1) * 6 * 16)
                for a in range(2):
                    pe.wait_ge(max_in[2 * hh + a], (i + 1) * PARTS * 16)
                    for p in range(PAIRS):
                        for kk in range(2):
                            for c in range(QC):
                                pass_2(h, hh, a, 2 * p + kk, c)
                            if not last:
                                pass_1(h + 1, 1 - hh, a, 2 * p + kk)
                        if p > 0:
                            if p == 1 and a == 0:
                                pe.wait_ge(v_ready, h + 1)
                            times_v(h, hh, a, p - 1)
                        elif a == 1:
                            times_v(h, hh, 0, PAIRS - 1)
                        elif not first:
                            times_v(h - 1, 1 - hh, 1, PAIRS - 1)

            each_head(pe, body)
            times_v(HEADS - 1, 1, 1, PAIRS - 1)

        @block.scalar
        def _(act):
            def body(i, hh, first, last):
                h = 2 * i + hh
                for a in range(2):
                    u = 2 * h + a
                    for e in range(EXPS):
                        pair, kk, c = e // (2 * QC), e // QC % 2, e % QC
                        if e % (2 * QC) == 0:
                            wait(act, pv_done, u * PAIRS + pair - SLOTS + 1)
                        act.wait_ge(st_done, u * EXPS + e + 1)
                        act.activation(probs[pair % SLOTS][:, kk, c * BANK:(c + 1) * BANK],
                                       st_ps[e % ST][:, :], ACT.Exp, scale=SCALE).then_inc(exp_done, 1)

            act.wait_ge(ffn_in, len(FFN) * 16)
            for name, of in zip(FFN, ints):
                act.copy(w[name][:, :, :], of[:, :, :]).then_inc(floats, 1)
            each_head(act, body)

        @block.vector
        def _(dve):
            dve.memset(o_ps[:, :], 0.0).then_inc(o_cleared, 1)
            for a in range(2):
                dve.memset(neg_max[a][:, :], 0.0).then_inc(cleared, 1)
            dve.wait_ge(cleared, 2)

            def maximum(h, a, r):
                u = 2 * h + a
                if r == 0:
                    wait(dve, unit_max, u - 1)
                dve.wait_ge(s_done, u * MAXES + r + 1)
                dve.tensor_reduce(tile_max[a][:, r // KW, r % KW:r % KW + 1], s_ps[r % 2][:, :],
                                  AX.X, ALU.max).then_inc(s_read, 1)

            def unit_maxima(h, a):
                u = 2 * h + a
                dve.wait_ge(s_read, (u + 1) * MAXES)
                wait(dve, max_turned, u - 1)
                dve.tensor_reduce(neg_max[a][:, 0:QT], tile_max[a][:, :, :], AX.X, ALU.max,
                                  negate=True).then_inc(unit_max, 1)
                dve.wait_ge(unit_max, u + 1)
                wait(dve, max_cut, CUTS * (u - 1))
                dve.transpose(neg_max_t[a][:, :], neg_max[a][:, :]).then_inc(max_turned, 1)

            def invert(h, a):
                dve.wait_ge(spread_in[a], (h + 1) * QC * 16)
                dve.reciprocal(spread[a][:, :], spread[a][:, :]).then_inc(inverted, 1)

            for a in range(2):
                for r in range(MAXES):
                    maximum(0, a, r)
                unit_maxima(0, a)

            def drain(h, a):
                u = 2 * h + a
                dve.wait_ge(pv_done, (u + 1) * PAIRS)
                wait(dve, whole_done, u - 1)
                dve.tensor_copy(sums[a][:, :], o_ps[:, :]).then_inc(sums_out, 1)

            def halve_weights():
                dve.wait_ge(floats, len(FFN))
                for name in FFN:
                    dve.tensor_scalar(w[name + "_half"][:, :, :], w[name][:, :, :], float(NARROW), float(-NARROW),
                                      ALU.min, ALU.max)

            def flag_wide():
                for n, name in enumerate(FFN):
                    for low in range(2):
                        dve.tensor_reduce(tops[:, 2 * n + low:2 * n + low + 1], w[name][:, :, :], AX.XY,
                                          ALU.min if low else ALU.max, negate=bool(low)).then_inc(topped, 1)
                dve.wait_ge(topped, 2 * len(FFN))
                dve.tensor_reduce(top[:, :], tops[:, :], AX.X, ALU.max).then_inc(topped, 1)
                dve.wait_ge(topped, 2 * len(FFN) + 1)
                dve.tensor_scalar(w["wide"][:, :], top[:, :], NARROW + 0.5, None, ALU.is_gt).then_inc(topped, 1)

            def body(i, hh, first, last):
                h = 2 * i + hh
                for a in range(2):
                    h_before, a_before = (h, 0) if a == 1 else (h - 1, 1)
                    any_before = a == 1 or not first
                    if last:
                        drain(h_before, a_before)
                        if a == 0:
                            halve_weights()
                        else:
                            flag_wide()
                        invert(h_before, a_before)
                        continue
                    for r in range(MAXES):
                        maximum(h + 1, a, r)
                        if any_before and r == 1:
                            drain(h_before, a_before)
                        if any_before and r == MAXES - 4:
                            invert(h_before, a_before)
                    unit_maxima(h + 1, a)

            each_head(dve, body)
            drain(HEADS - 1, 1)
            invert(HEADS - 1, 1)

        @block.gpsimd
        def _(pool):
            for i in range(2):
                wait(pool, ones_set, 2 * i)
                pool.memset(k2nd[i][STACK:ROWS, :], 1.0).then_inc(ones_set, 1)
                pool.wait_ge(ones_set, 2 * i + 1)
                pool.memset(v_head[i][:, :, HD:VM], 1.0).then_inc(ones_set, 1)
            pool.wait_ge(ones_set, 4)

            def cut(h, a):
                steps = CUTS * (2 * h + a)
                pool.wait_ge(max_turned, 2 * h + a + 1)
                wait(pool, max_out[a], h * 16)
                apart(pool, passed_pool)
                pool.tensor_copy(max_parts[a][:, 0, :], neg_max_t[a][:, :]).then_inc(max_cut, 1)
                pool.wait_ge(max_cut, steps + 1)
                pool.tensor_tensor(max_rest[:, :], neg_max_t[a][:, :], max_parts[a][:, 0, :],
                                   ALU.subtract).then_inc(max_cut, 1)
                pool.wait_ge(max_cut, steps + 2)
                apart(pool, passed_pool)
                pool.tensor_copy(max_parts[a][:, 1, :], max_rest[:, :]).then_inc(max_cut, 1)
                pool.wait_ge(max_cut, steps + 3)
                pool.tensor_tensor(max_parts[a][:, 2, :], max_rest[:, :], max_parts[a][:, 1, :],
                                   ALU.subtract).then_inc(max_cut, 1)

            def head_v(h, hh):
                wait(pool, pv_done, (h - 1) * 2 * PAIRS)
                apart(pool, passed_pool)
                pool.tensor_copy(v_head[hh][:, :, 0:HD],
                                 t["kept"][:, bass.ds(h, 1), :, :].rearrange("p h k d -> p (h k) d")
                                 ).then_inc(v_ready, 1)

            def add_odd(h, a):
                pool.wait_ge(sums_out, 2 * h + a + 1)
                pool.wait_ge(odd_in[a], (h + 1) * 16)
                wait(pool, kept[a], h * QC * 16)
                wait(pool, spread_in[a], h * QC * 16)
                pool.tensor_tensor(whole[a][:, :], sums[a][0:P // 2, :], odd[a][:, :],
                                   ALU.add).then_inc(whole_done, 1)

            head_v(0, 0)
            cut(0, 0)
            pool.memset(w["ones"][:, :], 1.0)
            pool.memset(w["ident"][:, :], 0.0).then_inc(ident_set, 1)
            pool.wait_ge(ident_set, 1)
            pool.affine_select(out=w["ident"][:, :], in_=w["ident"][:, :], compare_op=ALU.not_equal, fill=1.0,
                               base=0, pattern=[[-1, P]], channel_multiplier=1)

            def body(i, hh, first, last):
                h = 2 * i + hh
                cut(h, 1)
                if not first:
                    add_odd(h - 1, 1)
                if not last:
                    head_v(h + 1, 1 - hh)
                    cut(h + 1, 0)
                add_odd(h, 0)

            each_head(pool, body)
            add_odd(HEADS - 1, 1)


def finish(nc, t, w, B, T, D, HID):
    CH = BANK
    NCS = T // CH
    NCH = B * NCS
    TT = CH // P
    KD = D // P
    HD = D // N_HEAD
    HPT = P // HD
    HT = HID // P
    with ExitStack() as ctx:
        def sb(name, shape, dt=F32):
            return ctx.enter_context(nc.sbuf_tensor(name, shape, dt))

        def psum(name, shape):
            return ctx.enter_context(nc.psum_tensor(name, shape, F32))

        def sem(name):
            return ctx.enter_context(nc.semaphore(name))

        wide_count = sb("wide_count", [P, 1])
        wide_int = sb("wide_int", [1, 1], I32)
        hidden_factor = sb("hidden_factor", [P, 1])
        down_factor = sb("down_factor", [P, 1])
        heads = [sb(f"heads{i}", [P, KD, CH]) for i in range(2)]
        x_in = [sb(f"x_in{i}", [P, TT, D]) for i in range(2)]
        inverse = [sb(f"inverse{i}", [P, KD, CH]) for i in range(2)]
        z = sb("z", [P, TT, D])
        x1 = [sb(f"x1{i}", [P, TT, D]) for i in range(2)]
        x1_t = sb("x1_t", [P, KD, CH])
        x1_high = sb("x1_high", [P, KD, CH], F16)
        x1_low = sb("x1_low", [P, KD, CH], F16)
        silu = [sb(f"silu{i}", [P, CH]) for i in range(2)]
        hidden = sb("hidden", [P, HT, CH])
        h_high = sb("h_high", [P, HT, CH], F16)
        h_low = sb("h_low", [P, HT, CH], F16)
        y = [sb(f"y{i}", [P, TT, D]) for i in range(2)]
        result = [sb(f"result{i}", [P, TT, D]) for i in range(2)]
        stats = sb("stats", [P, 2 * TT, 6])
        moments = sb("moments", [P, 2 * TT, 2])
        var_eps = sb("var_eps", [P, 2 * TT])
        std = sb("std", [P, 2 * TT])
        rstd = sb("rstd", [P, 2 * TT])
        warm = sb("warm", [P, 1])

        t_ps = psum("t_ps", [P, KD, CH])
        p_ps = psum("p_ps", [P, TT, D])
        g_ps = [psum(f"g_ps{i}", [P, CH]) for i in range(2)]
        u_ps = [psum(f"u_ps{i}", [P, CH]) for i in range(2)]

        passed, passed_sp = sem("passed"), sem("passed_sp")
        wide_summed = sem("wide_summed")
        wide_known = sem("wide_known")
        factors = sem("factors")
        inverse_in = [sem(f"inverse_in{i}") for i in range(2)]
        softmaxed = sem("softmaxed")
        heads_in = [sem(f"heads_in{i}") for i in range(2)]
        x_landed = [sem(f"x_landed{i}") for i in range(2)]
        biased = sem("biased")
        proj_done = sem("proj_done")
        z_done = sem("z_done")
        z_stats = sem("z_stats")
        z_moments = sem("z_moments")
        y_stats = sem("y_stats")
        y_moments = sem("y_moments")
        var_done = sem("var_done")
        std_done = sem("std_done")
        rstd_done = sem("rstd_done")
        x1_done = sem("x1_done")
        turned = sem("turned")
        x1_high_done = sem("x1_high_done")
        x1_low_done = sem("x1_low_done")
        x1_t_done = sem("x1_t_done")
        gate_done = sem("gate_done")
        up_done = sem("up_done")
        silu_done = sem("silu_done")
        hidden_done = sem("hidden_done")
        h_high_done = sem("h_high_done")
        h_low_done = sem("h_low_done")
        last_low_done = sem("last_low_done")
        down_done = sem("down_done")
        y_done = sem("y_done")
        result_done = sem("result_done")
        kept = [sem(f"kept{i}") for i in range(2)]

        def each_chunk(eng, body):
            def turn(i, first, last):
                body(2 * i, 0, first, False)
                body(2 * i + 1, 1, False, last)
            turn(0, True, False)
            with eng.Fori(1, NCH // 2 - 1) as i:
                turn(i, False, False)
            turn(NCH // 2 - 1, False, True)

        def landed(c, par):
            return (c - par + 2) * 8

        heads_dram = t["heads"].rearrange("(b g p) n -> p b g n", b=B, p=P)

        block = ctx.enter_context(nc.Block())

        @block.sync
        def _(sp):
            def load(c, par):
                wait(sp, proj_done, 2 * (c - 1))
                apart(sp, passed_sp)
                sp.dma_start(heads[par][:, :, :], heads_dram[:, bass.ds(c // NCS, 1), :, bass.ds(c % NCS * CH, CH)]
                             .rearrange("p b g n -> p (b g) n")).then_inc(heads_in[par], 16)
                for kd in range(KD):
                    row = t["inverses"][bass.ds(c // NCS * N_HEAD + kd * HPT, HPT), bass.ds(c % NCS * CH, CH)]
                    sp.dma_start(inverse[par][:, kd, :],
                                 bass.AP(tensor=row.tensor, offset=row.offset, ap=[[T, HPT], [0, HD], [1, CH]])
                                 ).then_inc(inverse_in[par], 16)
                wait(sp, z_done, 2 * (c - 1))
                apart(sp, passed_sp)
                sp.dma_start(x_in[par][:, :, :], t["x"].rearrange("(n p) d -> p n d", p=P)
                             [:, bass.ds(c * TT, TT), :]).then_inc(x_landed[par], 16)

            load(0, 0)
            load(1, 1)

            def body(c, par, first, last):
                if not isinstance(c, int) or c + 2 < NCH:
                    load(c + 2, par)
                if not first and (not isinstance(c, int) or c > 1):
                    keep(c - 2, par)

            def keep(c, par):
                sp.wait_ge(result_done, c + 1)
                sp.dma_start(t["out"].rearrange("(n p) d -> p n d", p=P)[:, bass.ds(c * TT, TT), :],
                             result[par][:, :, :]).then_inc(kept[par], 16)

            each_chunk(sp, body)
            keep(NCH - 2, 0)
            keep(NCH - 1, 1)
            for par in range(2):
                sp.wait_ge(kept[par], NCH // 2 * 16)

        @block.tensor
        def _(pe):
            def output_projection(c, par):
                pe.wait_ge(softmaxed, c + 1)
                for n in range(TT):
                    if n % 2 == 0:
                        wait(pe, y_done, 2 * (c - 1) - 1 + n // 2)
                    for kd in range(KD):
                        mm = pe.matmul(p_ps[:, n, :], heads[par][:, kd, n * P:(n + 1) * P], w["w_out"][:, kd, :],
                                       start=kd == 0, stop=kd == KD - 1)
                    if n % 2 == 1:
                        mm.then_inc(proj_done, 1)

            def ffn(wide):
                def product(to, pairs, first, last):
                    for n, (stationary, moving) in enumerate(pairs):
                        mm = pe.matmul(to, stationary, moving, start=first and n == 0,
                                       stop=last and n == len(pairs) - 1)
                    return mm

                def project_in(name, to, m):
                    for kd in range(KD):
                        at = (slice(None), kd, slice(m * P, (m + 1) * P))
                        if wide:
                            pairs = [(w[name][at], x1_t[:, kd, :])]
                        else:
                            half = w[name + "_half"][at]
                            pairs = [(half, x1_high[:, kd, :]), (half, x1_low[:, kd, :])]
                        mm = product(to, pairs, kd == 0, kd == KD - 1)
                    return mm

                def body(c, par, first, last):
                    pe.wait_ge(x1_done, c + 1)
                    wait(pe, x1_t_done, KD * c)
                    for kd in range(KD):
                        for n in range(TT):
                            mm = pe.transpose(t_ps[:, kd, n * P:(n + 1) * P], x1[par][:, n, kd * P:(kd + 1) * P],
                                              w["ident"][:, :])
                        mm.then_inc(turned, 1)
                    if not last:
                        output_projection(c + 1, 1 - par)
                    pe.wait_ge(x1_low_done, KD * (c + 1))
                    for m in range(HT):
                        wait(pe, silu_done, c * HT + m - 1)
                        project_in("w_gate", g_ps[m % 2][:, :], m).then_inc(gate_done, 1)
                        wait(pe, hidden_done, c * HT + m - 1)
                        project_in("w_up", u_ps[m % 2][:, :], m).then_inc(up_done, 1)
                    if not last:
                        pe.wait_ge(z_done, 2 * (c + 2))
                    for tiles in ((0, TT // 2), (1,), (TT // 2 + 1,)):
                        for m in range(HT):
                            if tiles[0] == 0:
                                if m < HT - 1:
                                    pe.wait_ge(h_low_done, c * (HT - 1) + m + 1)
                                else:
                                    pe.wait_ge(last_low_done, c + 1)
                            for n in tiles:
                                at = (slice(None), m, slice(n * P, (n + 1) * P))
                                if wide:
                                    pairs = [(hidden[at], w["w_down"][:, m, :])]
                                else:
                                    half = w["w_down_half"][:, m, :]
                                    pairs = [(h_high[at], half), (h_low[at], half)]
                                mm = product(p_ps[:, n, :], pairs, m == 0, m == HT - 1)
                        if tiles[0] > 0:
                            mm.then_inc(down_done, 1)

                each_chunk(pe, body)

            pe.matmul(t_ps[:, 0, 0:1], w["ones"][:, :], w["wide"][:, :], start=True, stop=True
                      ).then_inc(wide_summed, 1)
            output_projection(0, 0)
            pe.wait_ge(wide_known, 2)
            wide = pe.value_load(wide_int[0:1, 0:1], min_val=0, max_val=P)
            with pe.If(wide > 0):
                ffn(True)
            with pe.Else():
                ffn(False)

        @block.scalar
        def _(act):
            def deviations(k):
                act.wait_ge(var_done, k + 1)
                wait(act, rstd_done, k)
                act.activation(std[:, :], var_eps[:, :], ACT.Sqrt).then_inc(std_done, 1)

            def load_silu():
                act.activation(warm[:, :], w["ones"][:, 0:1], ACT.Silu)

            def high(c, m):
                act.wait_ge(hidden_done, c * HT + m + 1)
                if m < HT - 1:
                    wait(act, h_low_done, (c - 1) * (HT - 1) + m + 1)
                else:
                    wait(act, last_low_done, c)
                act.copy(h_high[:, m, :], hidden[:, m, :]).then_inc(h_high_done, 1)

            act.wait_ge(wide_summed, 1)
            act.copy(wide_count[:, :], t_ps[:, 0, 0:1]).then_inc(wide_known, 1)
            act.wait_ge(wide_known, 1)
            act.copy(wide_int[:, :], wide_count[0:1, :]).then_inc(wide_known, 1)
            deviations(0)
            load_silu()

            def body(c, par, first, last):
                for kd in range(KD):
                    act.wait_ge(turned, KD * c + kd + 1)
                    act.activation(x1_t[:, kd, :], t_ps[:, kd, :], ACT.Copy, scale=X1_SCALE
                                   ).then_inc(x1_t_done, 1)
                    act.wait_ge(x1_t_done, KD * c + kd + 1)
                    act.copy(x1_high[:, kd, :], x1_t[:, kd, :]).then_inc(x1_high_done, 1)
                for m in range(HT):
                    act.wait_ge(gate_done, c * HT + m + 1)
                    wait(act, hidden_done, c * HT + m - 1)
                    act.activation(silu[m % 2][:, :], g_ps[m % 2][:, :], ACT.Silu,
                                   scale=QUANT_SCALE / X1_SCALE).then_inc(silu_done, 1)
                    if m > 0:
                        high(c, m - 1)
                high(c, HT - 1)
                deviations(c + 1)
                if not last:
                    load_silu()

            each_chunk(act, body)
            deviations(NCH + 1)

        @block.vector
        def _(dve):
            dve.wait_ge(wide_known, 1)
            dve.tensor_scalar(hidden_factor[:, :], wide_count[:, :], 0.0, WIDE_SCALE,
                              ALU.is_equal, ALU.max).then_inc(factors, 1)
            dve.tensor_scalar(down_factor[:, :], wide_count[:, :], 0.0, 1 / WIDE_SCALE,
                              ALU.is_gt, ALU.mult).then_inc(factors, 1)
            dve.wait_ge(factors, 2)
            dve.tensor_scalar(hidden_factor[:, :], hidden_factor[:, :], QUANT_SCALE / X1_SCALE * HIDDEN_SCALE,
                              None, ALU.mult).then_inc(factors, 1)
            dve.tensor_scalar(down_factor[:, :], down_factor[:, :], 1.0, QUANT_SCALE / HIDDEN_SCALE,
                              ALU.max, ALU.mult).then_inc(factors, 1)
            dve.wait_ge(factors, 4)
            dve.memset(moments[:, :, :], 1.0).then_inc(z_moments, 1)
            dve.wait_ge(z_moments, 1)

            def count(src, at, counted):
                for n in range(TT):
                    dve.bn_stats(stats[:, at + n, :], src[:, n, :]).then_inc(counted, 1)

            def average(at, n0, counted, averaged):
                dve.wait_ge(counted, TT * (n0 + 1))
                apart(dve, passed)
                for n in range(TT):
                    dve.bn_aggr(moments[:, at + n, :], stats[:, at + n, :]).then_inc(averaged, 1)

            def sum_z(c, par):
                dve.wait_ge(biased, c + 1)
                for j in range(2):
                    dve.wait_ge(proj_done, 2 * c + j + 1)
                    if j == 0:
                        wait(dve, x1_done, c)
                    dve.tensor_tensor(z[:, 2 * j:2 * j + 2, :], p_ps[:, 2 * j:2 * j + 2, :],
                                      x_in[par][:, 2 * j:2 * j + 2, :], ALU.add).then_inc(z_done, 1)

            def count_z(c):
                dve.wait_ge(z_done, 2 * c + 2)
                wait(dve, z_moments, 1 + TT * c)
                count(z, 0, z_stats)

            def average_z(c):
                wait(dve, var_done, c)
                average(0, c, z_stats, z_moments)

            def sum_y(c, par):
                for j in range(2):
                    dve.wait_ge(down_done, 2 * c + j + 1)
                    if j == 0:
                        wait(dve, result_done, c - 1)
                    dve.scalar_tensor_tensor(y[par][:, 2 * j:2 * j + 2, :], p_ps[:, 2 * j:2 * j + 2, :],
                                             down_factor[:, 0:1], x1[par][:, 2 * j:2 * j + 2, :],
                                             ALU.mult, ALU.add).then_inc(y_done, 1)

            def moments_y(c, par):
                dve.wait_ge(y_done, 2 * c + 2)
                wait(dve, y_moments, TT * c)
                wait(dve, var_done, c + 2)
                wait(dve, result_done, c)
                count(y[par], TT, y_stats)
                average(TT, c, y_stats, y_moments)

            def variances(k, zs, ys):
                dve.wait_ge(z_moments, 1 + TT * zs)
                wait(dve, y_moments, TT * ys)
                wait(dve, std_done, k)
                dve.tensor_scalar(var_eps[:, :], moments[:, :, 1], EPS, None, ALU.add).then_inc(var_done, 1)

            def invert(k, x1s, results):
                dve.wait_ge(std_done, k + 1)
                wait(dve, x1_done, x1s)
                wait(dve, result_done, results)
                dve.reciprocal(rstd[:, :], std[:, :]).then_inc(rstd_done, 1)
                dve.wait_ge(rstd_done, k + 1)

            def normalize(to, of, at, done):
                for n in range(TT):
                    last = dve.tensor_scalar(to[:, n, :], of[:, n, :], moments[:, at + n, 0:1],
                                             rstd[:, at + n:at + n + 1], ALU.subtract, ALU.mult)
                last.then_inc(done, 1)

            def hide(c, m):
                dve.wait_ge(silu_done, c * HT + m + 1)
                dve.wait_ge(up_done, c * HT + m + 1)
                if m < HT - 1:
                    wait(dve, h_low_done, (c - 1) * (HT - 1) + m + 1)
                else:
                    wait(dve, last_low_done, c)
                dve.scalar_tensor_tensor(hidden[:, m, :], u_ps[m % 2][:, :],
                                         hidden_factor[:, 0:1], silu[m % 2][:, :],
                                         ALU.mult, ALU.mult).then_inc(hidden_done, 1)

            def low_hidden(c):
                dve.wait_ge(h_high_done, (c + 1) * HT)
                dve.tensor_tensor(h_low[:, HT - 1, :], hidden[:, HT - 1, :], h_high[:, HT - 1, :],
                                  ALU.subtract).then_inc(last_low_done, 1)

            def low(c, kd):
                dve.wait_ge(x1_high_done, KD * c + kd + 1)
                dve.tensor_tensor(x1_low[:, kd, :], x1_t[:, kd, :], x1_high[:, kd, :],
                                  ALU.subtract).then_inc(x1_low_done, 1)

            def second_norm(c, par):
                wait(dve, kept[par], landed(c, par) - 16)
                normalize(result[par], y[par], TT, result_done)

            sum_z(0, 0)
            count_z(0)
            average_z(0)
            variances(0, 1, 0)
            invert(0, 0, 0)
            normalize(x1[0], z, 0, x1_done)

            def body(c, par, first, last):
                if not first:
                    sum_y(c - 1, 1 - par)
                for kd in range(KD):
                    low(c, kd)
                if not first:
                    if not isinstance(c, int) or c > 1:
                        second_norm(c - 2, par)
                    moments_y(c - 1, 1 - par)
                if not last:
                    sum_z(c + 1, 1 - par)
                hide(c, 0)
                if not last:
                    count_z(c + 1)
                hide(c, 1)
                if not last:
                    average_z(c + 1)
                variances(c + 1, NCH if last else c + 2, c)
                for m in range(2, HT):
                    hide(c, m)
                low_hidden(c)
                invert(c + 1, c + 1, c - 1)
                if not last:
                    normalize(x1[1 - par], z, 0, x1_done)

            each_chunk(dve, body)
            sum_y(NCH - 1, 1)
            second_norm(NCH - 2, 0)
            moments_y(NCH - 1, 1)
            variances(NCH + 1, NCH, NCH)
            invert(NCH + 1, NCH, NCH - 1)
            second_norm(NCH - 1, 1)

        @block.gpsimd
        def _(pool):
            def divide(c, par):
                pool.wait_ge(heads_in[par], landed(c, par))
                pool.wait_ge(inverse_in[par], KD * landed(c, par))
                pool.tensor_tensor(heads[par][:, :, :], heads[par][:, :, :], inverse[par][:, :, :],
                                   ALU.mult).then_inc(softmaxed, 1)

            def bias(c, par):
                pool.wait_ge(x_landed[par], landed(c, par))
                pool.tensor_tensor(x_in[par][:, :, :], x_in[par][:, :, :],
                                   w["b_out"][:, :].unsqueeze(1).broadcast_to([P, TT, D]), ALU.add).then_inc(biased, 1)

            for c in range(2):
                divide(c, c)
                bias(c, c)

            def body(c, par, first, last):
                if not isinstance(c, int) or c + 2 < NCH:
                    divide(c + 2, par)
                    bias(c + 2, par)
                for m in range(HT - 1):
                    pool.wait_ge(h_high_done, c * HT + m + 1)
                    pool.tensor_tensor(h_low[:, m, :], hidden[:, m, :], h_high[:, m, :],
                                       ALU.subtract).then_inc(h_low_done, 1)

            each_chunk(pool, body)


def layer(nc, t, B, T, D, HID):
    HD = D // N_HEAD
    HEADS = B * N_HEAD
    t["q_parts"] = nc.dram_tensor("q_parts", [HEADS, HD, PARTS, T], BF16).ap()
    t["k_parts"] = nc.dram_tensor("k_parts", [HEADS, HD, PARTS, T], BF16).ap()
    t["max_parts"] = nc.dram_tensor("max_parts_out", [4, P, PARTS, 32], BF16).ap()
    t["heads"] = nc.dram_tensor("heads_out", [HEADS * HD, T], F32).ap()
    t["inverses"] = nc.dram_tensor("inverses_out", [HEADS, T], F32).ap()
    with nc.sbuf_tensor("kept_v", [P, HEADS, T // P, HD], F32) as kept:
        t["kept"] = kept
        project(nc, t, B, T, D)
        with ExitStack() as ctx:
            def sb(name, shape, dt=F32):
                return ctx.enter_context(nc.sbuf_tensor(name, shape, dt))

            w = {"w_out": sb("w_out", [P, D // P, D]), "b_out": sb("b_out", [P, D]),
                 "ident": sb("ident", [P, P]), "ones": sb("ones", [P, P]),
                 "wide": sb("wide", [P, 1])}
            for name, rows, columns in (("w_gate", D, HID), ("w_up", D, HID), ("w_down", HID, D)):
                w[name] = sb(name, [P, rows // P, columns])
                w[name + "_half"] = sb(name + "_half", [P, rows // P, columns], F16)
            attend(nc, t, w, B, T, D)
            finish(nc, t, w, B, T, D, HID)


def rotary_tables(T, hd, rows):
    inv = (np.float32(1.0) / np.float32(10000.0) ** (np.arange(0, hd, 2, dtype=np.float32) / np.float32(hd)))
    angle = np.repeat(np.arange(T, dtype=np.float32)[:, None] * inv.astype(np.float32)[None, :], 2, axis=1).T
    sign = np.where(np.arange(hd) % 2 == 0, -1.0, 1.0).astype(np.float32)[:, None]
    return (np.ascontiguousarray(np.tile(np.cos(angle), (rows // hd, 1)), np.float32),
            np.ascontiguousarray(np.tile(np.sin(angle) * sign, (rows // hd, 1)), np.float32))


def kernel(L0_attn_x, L0_attn_w_qkv, L0_attn_b_qkv, L0_attn_w_out, L0_attn_b_out,
           L0_ffn_w_gate, L0_ffn_w_up, L0_ffn_w_down):
    import concourse.bacc as bacc
    from concourse.bass_utils import run_bass_kernel_spmd

    x = np.asarray(L0_attn_x)
    B, T, D = x.shape
    HID = L0_ffn_w_gate.shape[0]
    cos, sin = rotary_tables(T, D // N_HEAD, P)
    flat = x.reshape(B * T, D)
    arrays = {
        "x": np.ascontiguousarray(flat),
        "x_t": np.ascontiguousarray(flat.T),
        "w_qkv": np.ascontiguousarray(L0_attn_w_qkv),
        "b_qkv": np.ascontiguousarray(L0_attn_b_qkv),
        "b_qkv_cols": np.ascontiguousarray(np.asarray(L0_attn_b_qkv).reshape(3 * D // P, P).T),
        "w_out": np.ascontiguousarray(L0_attn_w_out),
        "b_out": np.ascontiguousarray(L0_attn_b_out),
        "w_gate": np.ascontiguousarray(np.asarray(L0_ffn_w_gate).T),
        "w_up": np.ascontiguousarray(np.asarray(L0_ffn_w_up).T),
        "w_down": np.ascontiguousarray(np.asarray(L0_ffn_w_down).T),
        "cos": cos,
        "sin": sin,
    }
    nc = bacc.Bacc("TRN2", target_bir_lowering=False, num_devices=1)
    t = {n: nc.dram_tensor("in_" + n, a.shape, mybir.dt.from_np(a.dtype), kind="ExternalInput").ap()
         for n, a in arrays.items()}
    t["out"] = nc.dram_tensor("out", (B * T, D), F32, kind="ExternalOutput").ap()
    layer(nc, t, B, T, D, HID)
    r = run_bass_kernel_spmd(nc, [{"in_" + n: a for n, a in arrays.items()}], core_ids=[0])
    return r.results[0]["out"].reshape(B, T, D)
```

```python
from contextlib import ExitStack

import numpy as np

import concourse.bass as bass
from concourse import mybir

P = 128
N_HEAD = 16
FFN = ("w_gate", "w_up", "w_down")
PARTS = 3
BANK = 512
EPS = 1e-5
QUANT_SCALE = float(np.float32(1.0 / 127.0))
NARROW = 127
X1_SCALE = 2.0 ** 11
HIDDEN_SCALE = 2.0 ** -1
WIDE_SCALE = 2.0 ** -49

F32 = mybir.dt.float32
BF16 = mybir.dt.bfloat16
F16 = mybir.dt.float16
I32 = mybir.dt.int32
ACT = mybir.ActivationFunctionType
ALU = mybir.AluOpType
AX = mybir.AxisListType


def wait(eng, sem, value):
    if not isinstance(value, int) or value > 0:
        eng.wait_ge(sem, value)


def apart(eng, passed):
    eng.sem_inc(passed, 1)


def load_stacks(sp, t, h, q_to, k_to, landed):
    heads, HD, parts, T = t["q_parts"].shape

    def rows(source, part, n, step):
        head = source[bass.ds(h, 1), :, :, :]
        return bass.AP(tensor=head.tensor, offset=head.offset + part * T,
                       ap=[[step, n], [parts * T, HD], [1, T]])
    at = 0
    for part, n in ((0, 3), (1, 2), (2, 1)):
        sp.dma_start(q_to[at:at + n * HD, :], rows(t["q_parts"], part, n, 0)).then_inc(landed, 16)
        at += n * HD
    at = 0
    for n in (3, 2, 1):
        sp.dma_start(k_to[at:at + n * HD, :], rows(t["k_parts"], 0, n, T)).then_inc(landed, 16)
        at += n * HD


def project(nc, t, s, B, T, D):
    CH = BANK
    NC = T // CH
    CHUNKS = B * NC
    KD = D // P
    M = 2 * KD
    HALVES = [slice(0, KD), slice(KD, M)]
    HPT = P // (D // N_HEAD)
    HD = D // N_HEAD
    swap = [p ^ 1 for p in range(32)]
    with ExitStack() as ctx:
        def sb(name, shape, dt):
            return ctx.enter_context(nc.sbuf_tensor(name, shape, dt))

        def sem(name):
            return ctx.enter_context(nc.semaphore(name))

        w_qkv = sb("w_qkv", [P, KD, 3 * D], F32)
        bias_qk = sb("bias_qk", [P, 3 * KD], F32)
        cos = sb("cos", [P, T], F32)
        sin = sb("sin", [P, T], F32)
        x_t = [sb(f"x_t{i}", [P, KD, CH], F32) for i in range(2)]
        raw = [sb(f"raw{i}", [P, M, CH], F32) for i in range(2)]
        turned = [sb(f"turned{i}", [P, M, CH], F32) for i in range(2)]
        roped = [sb(f"roped{i}", [P, M, CH], F32) for i in range(2)]
        parts, stored = s["parts"], s["stored"]
        rest = turned
        qk_ps = [ctx.enter_context(nc.psum_tensor(f"qk_ps{m}", [P, CH], F32)) for m in range(M)]
        v_ps = [ctx.enter_context(nc.psum_tensor(f"v_ps{n}", [P, 2, D], F32)) for n in range(2)]

        passed, passed_sp = sem("passed"), sem("passed_sp")
        weights_in = sem("weights_in")
        bias_in = sem("bias_in")
        tables_in = sem("tables_in")
        x_in = [sem(f"x_in{i}") for i in range(2)]
        qk_done = sem("qk_done")
        v_done = sem("v_done")
        raw_done = sem("raw_done")
        v_kept = sem("v_kept")
        swapped = sem("swapped")
        cosined = sem("cosined")
        sined = sem("sined")
        roped_done = sem("roped_done")
        part1_done = sem("part1_done")
        rest_done = sem("rest_done")
        part2_done = sem("part2_done")
        part3_done = sem("part3_done")
        last_part3_done = sem("last_part3_done")

        block = ctx.enter_context(nc.Block())

        def each_sequence(eng, body):
            def turn(b):
                for c in range(NC):
                    body(b, c)
            turn(0)
            if B > 2:
                with eng.Fori(1, B - 1) as b:
                    turn(b)
            turn(B - 1)

        def exists(k):
            return not isinstance(k, int) or 0 <= k < CHUNKS

        @block.sync
        def _(sp):
            def load(k, i):
                wait(sp, v_done, (k - 1) * 2)
                sp.dma_start(x_t[i][:, :, :],
                             t["x_t"].rearrange("(k p) n -> p k n", p=P)[:, :, bass.ds(k * CH, CH)]
                             ).then_inc(x_in[i], 16)

            def store(b, c, last=False):
                for half, to in enumerate((t["q_parts"], t["k_parts"])):
                    if last:
                        sp.wait_ge(last_part3_done, half + 1)
                    else:
                        sp.wait_ge(part3_done, (b * NC + c) * 2 + half + 1)
                    to = to.rearrange("h d a n -> (h d) a n")
                    for m in range(KD):
                        row = (b * N_HEAD + m * HPT) * HD
                        sp.dma_start(to[bass.ds(row, P), :, c * CH:(c + 1) * CH],
                                     parts[c % 2][:, half * KD + m, :, :]).then_inc(stored[c % 2], 16)

            def body(b, c):
                k = b * NC + c
                if exists(k + 2):
                    load(k + 2, c % 2)
                if exists(k - 1):
                    apart(sp, passed_sp)
                    store(*((b, c - 1) if c > 0 else (b - 1, NC - 1)))
                if isinstance(b, int) and (b, c) == (B - 1, NC - 2):
                    for i in range(2):
                        sp.wait_ge(stored[i], NC // 2 * M * 16)
                    for h in range(2):
                        load_stacks(sp, t, h, s["q1st"][h], s["k1st"][h], s["first_in"][h])

            def weights(columns):
                sp.dma_start(w_qkv[:, :, columns], t["w_qkv"].rearrange("(k p) n -> p k n", p=P)[:, :, columns]
                             ).then_inc(weights_in, 16)

            weights(slice(0, P))
            load(0, 0)
            weights(slice(P, 3 * D))
            sp.dma_start(sin[:, :], t["sin"]).then_inc(tables_in, 16)
            sp.dma_start(cos[:, :], t["cos"]).then_inc(tables_in, 16)
            load(1, 1)
            each_sequence(sp, body)
            store(B - 1, NC - 1, last=True)

        @block.tensor
        def _(pe):
            def body(b, c):
                k = b * NC + c
                x = x_t[c % 2]
                pe.wait_ge(x_in[c % 2], (b * (NC // 2) + c // 2 + 1) * 16)
                for m in range(M):
                    if isinstance(k, int) and (k, m) == (0, 1):
                        pe.wait_ge(weights_in, 2 * 16)
                    wait(pe, raw_done, (k - 1) * M + m + 1)
                    for kd in range(KD):
                        mm = pe.matmul(qk_ps[m][:, :], w_qkv[:, kd, m * P:(m + 1) * P], x[:, kd, :],
                                       start=kd == 0, stop=kd == KD - 1)
                    mm.then_inc(qk_done, 1)
                for n in range(2):
                    wait(pe, v_kept, (k - 1) * 2 + n + 1)
                    for j in range(2):
                        at = (2 * n + j) * P
                        for kd in range(KD):
                            mm = pe.matmul(v_ps[n][:, j, :], x[:, kd, at:at + P], w_qkv[:, kd, 2 * D:3 * D],
                                           start=kd == 0, stop=kd == KD - 1)
                    mm.then_inc(v_done, 1)

            pe.wait_ge(weights_in, 16)
            each_sequence(pe, body)


        @block.scalar
        def _(act):
            def evacuate(k, i, m):
                act.wait_ge(qk_done, k * M + m + 1)
                if m % KD == 0:
                    wait(act, cosined, 2 * (k - 2) + m // KD + 1)
                act.activation(raw[i][:, m, :], qk_ps[m][:, :], ACT.Identity,
                               bias=bias_qk[:, m:m + 1]).then_inc(raw_done, 1)

            def keep_v(b, c, n):
                act.wait_ge(v_done, (b * NC + c) * 2 + n + 1)
                kt = c * (CH // P) + 2 * n
                act.copy(t["kept"][:, bass.ds(b * N_HEAD, N_HEAD), kt:kt + 2, :]
                         .rearrange("p h k d -> p k h d"),
                         v_ps[n][:, :, :].rearrange("p k (h d) -> p k h d", d=HD)).then_inc(v_kept, 1)

            def part_1(k, i, half):
                act.wait_ge(roped_done, 2 * k + half + 1)
                if half == 0:
                    wait(act, stored[i], (k - i) * 8 * M)
                at = HALVES[half]
                act.activation(parts[i][:, at, 0, :], roped[i][:, at, :], ACT.Copy).then_inc(part1_done, 1)

            def part_2(k, i, half):
                act.wait_ge(rest_done, 2 * k + half + 1)
                at = HALVES[half]
                act.activation(parts[i][:, at, 1, :], rest[i][:, at, :], ACT.Copy).then_inc(part2_done, 1)

            def body(b, c):
                k = b * NC + c
                i = c % 2
                ahead = exists(k + 1)
                b_next, c_next = (b, c + 1) if c + 1 < NC else (b + 1, 0)
                if ahead:
                    evacuate(k + 1, 1 - i, 0)
                    evacuate(k + 1, 1 - i, 1)
                    evacuate(k + 1, 1 - i, 2)
                if exists(k - 1):
                    part_2(k - 1, 1 - i, 0)
                if ahead:
                    evacuate(k + 1, 1 - i, 3)
                if exists(k - 1):
                    part_2(k - 1, 1 - i, 1)
                part_1(k, i, 0)
                if ahead:
                    keep_v(b_next, c_next, 0)
                part_1(k, i, 1)
                if ahead:
                    keep_v(b_next, c_next, 1)

            act.dma_start(bias_qk[:, :], t["b_qkv_cols"]).then_inc(bias_in, 16)
            act.wait_ge(bias_in, 16)
            for m in range(M):
                evacuate(0, 0, m)
            for n in range(2):
                keep_v(0, 0, n)
            each_sequence(act, body)
            for half in range(2):
                part_2(CHUNKS - 1, 1, half)

        @block.vector
        def _(dve):
            def cut(k, i, half):
                at = HALVES[half]
                dve.wait_ge(part1_done, 2 * k + half + 1)
                dve.tensor_tensor(rest[i][:, at, :], roped[i][:, at, :], parts[i][:, at, 0, :],
                                  ALU.subtract).then_inc(rest_done, 1)

            def body(b, c):
                k = b * NC + c
                i = c % 2
                for half, at in enumerate(HALVES):
                    for m in range(half * KD, (half + 1) * KD):
                        dve.wait_ge(raw_done, k * M + m + 1)
                        if m % KD == 0:
                            wait(dve, part3_done, 2 * (k - 2) + half + 1)
                        apart(dve, passed)
                        shuffle = dve.stream_shuffle(turned[i][:, m, :], raw[i][:, m, :], swap)
                    shuffle.then_inc(swapped, 1)
                    if isinstance(k, int) and (k, half) == (0, 0):
                        dve.wait_ge(tables_in, 2 * 16)
                    wait(dve, rest_done, 2 * (k - 2) + half + 1)
                    dve.tensor_tensor(roped[i][:, at, :], raw[i][:, at, :],
                                      cos[:, c * CH:(c + 1) * CH].unsqueeze(1).broadcast_to([P, KD, CH]),
                                      ALU.mult).then_inc(cosined, 1)
                if exists(k - 1):
                    for half in range(2):
                        cut(k - 1, 1 - i, half)
                for half, at in enumerate(HALVES):
                    dve.wait_ge(cosined, 2 * k + half + 1)
                    dve.wait_ge(sined, 2 * k + half + 1)
                    dve.tensor_tensor(roped[i][:, at, :], roped[i][:, at, :], turned[i][:, at, :],
                                      ALU.add).then_inc(roped_done, 1)

            each_sequence(dve, body)
            for half in range(2):
                cut(CHUNKS - 1, 1, half)
            for half, at in enumerate(HALVES):
                dve.wait_ge(part2_done, 2 * (CHUNKS - 1) + half + 1)
                dve.tensor_tensor(parts[1][:, at, 2, :], rest[1][:, at, :], parts[1][:, at, 1, :],
                                  ALU.subtract).then_inc(last_part3_done, 1)

        @block.gpsimd
        def _(pool):
            def part_3(k, i):
                for half, at in enumerate(HALVES):
                    pool.wait_ge(part2_done, 2 * k + half + 1)
                    pool.tensor_tensor(parts[i][:, at, 2, :], rest[i][:, at, :], parts[i][:, at, 1, :],
                                       ALU.subtract).then_inc(part3_done, 1)

            def body(b, c):
                k = b * NC + c
                i = c % 2
                for half, at in enumerate(HALVES):
                    pool.wait_ge(swapped, 2 * k + half + 1)
                    pool.tensor_tensor(turned[i][:, at, :], turned[i][:, at, :],
                                       sin[:, c * CH:(c + 1) * CH].unsqueeze(1).broadcast_to([P, KD, CH]),
                                       ALU.mult).then_inc(sined, 1)
                if exists(k - 1):
                    part_3(k - 1, 1 - i)

            pool.wait_ge(tables_in, 2 * 16)
            each_sequence(pool, body)


def norm_state(ctx, nc, t, B, T, D):
    KD = D // P
    TT = BANK // P
    free = t["kept"][:, :, :, :].rearrange("p h k d -> p (h k d)")
    taken = 0

    def place(outer):
        nonlocal taken
        taken += KD * BANK
        return free[:, taken - KD * BANK:taken].rearrange("p (a b) -> p a b", a=outer)

    def sb(name, shape, dt=F32):
        return ctx.enter_context(nc.sbuf_tensor(name, shape, dt))

    def sem(name):
        return ctx.enter_context(nc.semaphore(name))

    return dict(
        heads=[place(KD) for i in range(2)],
        inverse=[place(KD) for i in range(2)],
        x_in=[place(TT) for i in range(2)],
        z=place(TT),
        x1=[place(TT) for i in range(2)],
        stats=sb("stats", [P, 2 * TT, 6]),
        moments=sb("moments", [P, 2 * TT, 2]),
        var_eps=sb("var_eps", [P, 2 * TT]),
        std=sb("std", [P, 2 * TT]),
        rstd=sb("rstd", [P, 2 * TT]),
        wide_count=sb("wide_count", [P, 1]),
        wide_int=sb("wide_int", [1, 1], I32),
        hidden_factor=sb("hidden_factor", [P, 1]),
        down_factor=sb("down_factor", [P, 1]),
        passed=sem("passed_dve"), passed_sp=sem("passed_load"),
        wide_summed=sem("wide_summed"),
        wide_known=sem("wide_known"),
        factors=sem("factors"),
        heads_in=[sem(f"heads_in{i}") for i in range(2)],
        inverse_in=[sem(f"inverse_in{i}") for i in range(2)],
        x_landed=[sem(f"x_landed{i}") for i in range(2)],
        softmaxed=sem("softmaxed"),
        biased=sem("biased"),
        proj_done=sem("proj_done"),
        z_done=sem("z_done"),
        z_stats=sem("z_stats"),
        z_moments=sem("z_moments"),
        var_done=sem("var_done"),
        std_done=sem("std_done"),
        rstd_done=sem("rstd_done"),
        x1_done=sem("x1_done"),
        y_done=sem("y_done"),
        y_moments=sem("y_moments"),
        result_done=sem("result_done"))


def norm_steps(nc, t, w, f, B, T, D):
    CH = BANK
    NCS = T // CH
    TT = CH // P
    KD = D // P
    HD = D // N_HEAD
    HPT = P // HD
    heads_dram = t["heads"].rearrange("(b g p) n -> p b g n", b=B, p=P)

    def landed(c, par):
        return (c - par + 2) * 8

    def load(sp, c, par):
        wait(sp, f["proj_done"], 2 * (c - 1))
        apart(sp, f["passed_sp"])
        sp.dma_start(f["heads"][par][:, :, :], heads_dram[:, bass.ds(c // NCS, 1), :, bass.ds(c % NCS * CH, CH)]
                     .rearrange("p b g n -> p (b g) n")).then_inc(f["heads_in"][par], 16)
        for kd in range(KD):
            row = t["inverses"][bass.ds(c // NCS * N_HEAD + kd * HPT, HPT), bass.ds(c % NCS * CH, CH)]
            sp.dma_start(f["inverse"][par][:, kd, :],
                         bass.AP(tensor=row.tensor, offset=row.offset, ap=[[T, HPT], [0, HD], [1, CH]])
                         ).then_inc(f["inverse_in"][par], 16)
        wait(sp, f["z_done"], 2 * (c - 1))
        apart(sp, f["passed_sp"])
        sp.dma_start(f["x_in"][par][:, :, :], t["x"].rearrange("(n p) d -> p n d", p=P)
                     [:, bass.ds(c * TT, TT), :]).then_inc(f["x_landed"][par], 16)

    def divide(pool, c, par):
        pool.wait_ge(f["heads_in"][par], landed(c, par))
        pool.wait_ge(f["inverse_in"][par], KD * landed(c, par))
        pool.tensor_tensor(f["heads"][par][:, :, :], f["heads"][par][:, :, :], f["inverse"][par][:, :, :],
                           ALU.mult).then_inc(f["softmaxed"], 1)

    def bias(pool, c, par):
        pool.wait_ge(f["x_landed"][par], landed(c, par))
        pool.tensor_tensor(f["x_in"][par][:, :, :], f["x_in"][par][:, :, :],
                           w["b_out"][:, :].unsqueeze(1).broadcast_to([P, TT, D]), ALU.add
                           ).then_inc(f["biased"], 1)

    def output_projection(pe, c, par, to, tiles=range(TT)):
        if 0 in tiles:
            pe.wait_ge(f["softmaxed"], c + 1)
        for n in tiles:
            if n % 2 == 0:
                wait(pe, f["y_done"], 2 * (c - 1) - 1 + n // 2)
            for kd in range(KD):
                mm = pe.matmul(to[:, n, :], f["heads"][par][:, kd, n * P:(n + 1) * P], w["w_out"][:, kd, :],
                               start=kd == 0, stop=kd == KD - 1)
            if n % 2 == 1:
                mm.then_inc(f["proj_done"], 1)

    def sum_z(dve, c, par, product):
        dve.wait_ge(f["biased"], c + 1)
        for j in range(2):
            dve.wait_ge(f["proj_done"], 2 * c + j + 1)
            if j == 0:
                wait(dve, f["x1_done"], c)
            dve.tensor_tensor(f["z"][:, 2 * j:2 * j + 2, :], product[:, 2 * j:2 * j + 2, :],
                              f["x_in"][par][:, 2 * j:2 * j + 2, :], ALU.add).then_inc(f["z_done"], 1)

    def count(dve, src, at, counted):
        for n in range(TT):
            dve.bn_stats(f["stats"][:, at + n, :], src[:, n, :]).then_inc(counted, 1)

    def average(dve, at, n0, counted, averaged):
        dve.wait_ge(counted, TT * (n0 + 1))
        apart(dve, f["passed"])
        for n in range(TT):
            dve.bn_aggr(f["moments"][:, at + n, :], f["stats"][:, at + n, :]).then_inc(averaged, 1)

    def count_z(dve, c):
        dve.wait_ge(f["z_done"], 2 * c + 2)
        wait(dve, f["z_moments"], 1 + TT * c)
        count(dve, f["z"], 0, f["z_stats"])

    def average_z(dve, c):
        wait(dve, f["var_done"], c)
        average(dve, 0, c, f["z_stats"], f["z_moments"])

    def variances(dve, k, zs, ys):
        dve.wait_ge(f["z_moments"], 1 + TT * zs)
        wait(dve, f["y_moments"], TT * ys)
        wait(dve, f["std_done"], k)
        dve.tensor_scalar(f["var_eps"][:, :], f["moments"][:, :, 1], EPS, None, ALU.add
                          ).then_inc(f["var_done"], 1)

    def deviations(act, k):
        act.wait_ge(f["var_done"], k + 1)
        wait(act, f["rstd_done"], k)
        act.activation(f["std"][:, :], f["var_eps"][:, :], ACT.Sqrt).then_inc(f["std_done"], 1)

    def invert(dve, k, x1s, results):
        dve.wait_ge(f["std_done"], k + 1)
        wait(dve, f["x1_done"], x1s)
        wait(dve, f["result_done"], results)
        dve.reciprocal(f["rstd"][:, :], f["std"][:, :]).then_inc(f["rstd_done"], 1)
        dve.wait_ge(f["rstd_done"], k + 1)

    def normalize(dve, to, of, at, done):
        for n in range(TT):
            last = dve.tensor_scalar(to[:, n, :], of[:, n, :], f["moments"][:, at + n, 0:1],
                                     f["rstd"][:, at + n:at + n + 1], ALU.subtract, ALU.mult)
        last.then_inc(done, 1)

    return dict(landed=landed, load=load, divide=divide, bias=bias, sum_z=sum_z, count=count,
                           output_projection=output_projection, average=average, count_z=count_z,
                           average_z=average_z, variances=variances, deviations=deviations, invert=invert,
                           normalize=normalize)


def unit_state(ctx, nc, T):
    def sb(name, shape):
        return [ctx.enter_context(nc.sbuf_tensor(f"{name}{i}", shape, F32)) for i in range(2)]

    def sem(name):
        return ctx.enter_context(nc.semaphore(name))

    return dict(
        sums=sb("sums", [P, BANK]),
        odd=sb("odd", [P // 2, BANK]),
        whole=sb("whole", [P // 2, BANK]),
        spread=sb("spread", [P, T // 2 // P]),
        passed=sem("passed_unit"),
        sums_out=sem("sums_out"),
        odd_in=[sem(f"odd_in{i}") for i in range(2)],
        whole_done=sem("whole_done"),
        kept=[sem(f"kept{i}") for i in range(2)],
        spread_in=[sem(f"spread_in{i}") for i in range(2)],
        inverted=sem("inverted"),
        inverses_out=[sem(f"inverses_out{i}") for i in range(2)])


def unit_steps(t, u, T, D):
    HD = D // N_HEAD
    HALF = T // 2
    QC = HALF // BANK

    def odd_rows(sp, h, a):
        sp.wait_ge(u["sums_out"], 2 * h + a + 1)
        apart(sp, u["passed"])
        wait(sp, u["whole_done"], 2 * h + a - 1)
        apart(sp, u["passed"])
        sp.dma_start(u["odd"][a][:, :], u["sums"][a][P // 2:P, :]).then_inc(u["odd_in"][a], 16)

    def add_odd(pool, h, a):
        pool.wait_ge(u["sums_out"], 2 * h + a + 1)
        pool.wait_ge(u["odd_in"][a], (h + 1) * 16)
        wait(pool, u["kept"][a], h * QC * 16)
        wait(pool, u["spread_in"][a], h * QC * 16)
        pool.tensor_tensor(u["whole"][a][:, :], u["sums"][a][0:P // 2, :], u["odd"][a][:, :],
                           ALU.add).then_inc(u["whole_done"], 1)

    def keep(sp, h, a):
        sp.wait_ge(u["whole_done"], 2 * h + a + 1)
        apart(sp, u["passed"])
        for c in range(QC):
            at = a * HALF + c * BANK
            sp.dma_start(t["heads"][bass.ds(h * HD, HD), at:at + BANK],
                         u["whole"][a][c * 32:c * 32 + HD, :]).then_inc(u["kept"][a], 16)
        wait(sp, u["inverses_out"][a], h * 16)
        apart(sp, u["passed"])
        for c in range(QC):
            sp.dma_start(u["spread"][a][c * P // QC:(c + 1) * P // QC, :],
                         u["whole"][a][c * 32 + HD:c * 32 + HD + 1, :].rearrange("o (p n) -> o p n", p=P // QC)
                         ).then_inc(u["spread_in"][a], 16)

    def invert(dve, h, a):
        dve.wait_ge(u["spread_in"][a], (h + 1) * QC * 16)
        dve.reciprocal(u["spread"][a][:, :], u["spread"][a][:, :]).then_inc(u["inverted"], 1)

    def inverses(sp, h, a):
        sp.wait_ge(u["inverted"], 2 * h + a + 1)
        apart(sp, u["passed"])
        sp.dma_start(t["inverses"][bass.ds(h, 1), a * HALF:(a + 1) * HALF]
                     .rearrange("h (p n) -> (h p) n", p=P), u["spread"][a][:, :]
                     ).then_inc(u["inverses_out"][a], 16)

    return dict(odd_rows=odd_rows, add_odd=add_odd, keep=keep, invert=invert, inverses=inverses,
                           **u)


def attend(nc, t, w, s, f, u, B, T, D):
    HD = D // N_HEAD
    HEADS = B * N_HEAD
    HALF = T // 2
    KT = T // P
    PAIRS = KT // 2
    QC = HALF // BANK
    QT = HALF // P
    EXPS = KT * QC
    WIDE = 2 * BANK
    KW = T // WIDE
    MAXES = QT * KW
    ST = 3
    SLOTS = 4
    STACK = 6 * HD
    ROWS = STACK + PARTS
    CUTS = 4
    VM = HD + 1
    SCALE = float(HD) ** -0.5
    assert QC == 2 and KW * QT == KT and MAXES == KT
    with ExitStack() as ctx:
        def sb(name, shape, dt):
            return ctx.enter_context(nc.sbuf_tensor(name, shape, dt))

        def psum(name, shape):
            return ctx.enter_context(nc.psum_tensor(name, shape, F32))

        def sem(name):
            return ctx.enter_context(nc.semaphore(name))

        steps = norm_steps(nc, t, w, f, B, T, D)
        out = unit_steps(t, u, T, D)
        q1st, k1st, first_in = s["q1st"], s["k1st"], s["first_in"]
        q2nd = [sb(f"q2nd{i}", [ROWS, T], BF16) for i in range(2)]
        k2nd = [sb(f"k2nd{i}", [ROWS, T], BF16) for i in range(2)]
        v_head = [sb(f"v_head{i}", [P, KT, VM], F32) for i in range(2)]
        probs = [sb(f"probs{i}", [P, 2, HALF], F32) for i in range(SLOTS)]
        tile_max = [sb(f"tile_max{i}", [P, QT, KW], F32) for i in range(2)]
        neg_max = [sb(f"neg_max{i}", [P, 32], F32) for i in range(2)]
        neg_max_t = [sb(f"neg_max_t{i}", [P, 32], F32) for i in range(2)]
        max_parts = [sb(f"max_parts{i}", [P, PARTS, 32], BF16) for i in range(2)]
        max_rest = sb("max_rest", [P, 32], F32)
        st_ps = [psum(f"st_ps{i}", [P, BANK]) for i in range(ST)]
        s_ps = [psum(f"s_ps{i}", [P, WIDE]) for i in range(2)]
        o_ps = psum("o_ps", [P, BANK])
        TT = WIDE // D
        p_first = s_ps[0][:, :].rearrange("p (n d) -> p n d", n=TT)

        passed_sp, passed_pool = sem("passed_sp"), sem("passed_pool")
        ones_set = sem("ones_set")
        all_ones = sem("all_ones")
        b_spread = sem("b_spread")
        bias_done = sem("bias_done")
        bias_added = sem("bias_added")
        o_cleared = sem("o_cleared")
        second_in = [sem(f"second_in{i}") for i in range(2)]
        max_in = [sem(f"max_in{i}") for i in range(4)]
        max_out = [sem(f"max_out{i}") for i in range(2)]
        v_ready = sem("v_ready")
        s_done = sem("s_done")
        s_read = sem("s_read")
        unit_max = sem("unit_max")
        max_turned = sem("max_turned")
        max_cut = sem("max_cut")
        cleared = sem("cleared")
        st_done = sem("st_done")
        exp_done = sem("exp_done")
        pv_done = sem("pv_done")

        def each_head(eng, body):
            def turn(i, first, last):
                body(i, 0, first, False)
                body(i, 1, False, last)
            turn(0, True, False)
            with eng.Fori(1, HEADS // 2 - 1) as i:
                turn(i, False, False)
            turn(HEADS // 2 - 1, False, True)

        def before(e, ring):
            return e - ring if e >= ring else max(j for j in range(EXPS) if j % ring == e) - EXPS

        sums, sums_out, whole_done = out["sums"], out["sums_out"], out["whole_done"]
        kept, inverses_out = out["kept"], out["inverses_out"]

        tops = sb("tops", [P, 2 * len(FFN)], F32)
        top = sb("top", [P, 1], F32)
        ffn_in = sem("ffn_in")
        out_in = sem("out_in")
        floats = sem("floats")
        topped = sem("topped")
        ident_set = sem("ident_set")

        block = ctx.enter_context(nc.Block())

        @block.sync
        def _(sp):
            def maxima(h, hh, a):
                sp.wait_ge(max_cut, CUTS * (2 * h + a + 1))
                apart(sp, passed_sp)
                wait(sp, st_done, (2 * (h - 2) + a + 1) * EXPS)
                four = 2 * hh + a
                there = t["max_parts"][four]
                sp.dma_start(there, max_parts[a][:, :, :]).then_inc(max_out[a], 16)
                sp.wait_ge(max_out[a], (h + 1) * 16)
                for part in range(PARTS):
                    rows = bass.AP(tensor=there.tensor, offset=there.offset + part * 32,
                                   ap=[[PARTS * 32, QT], [32 * PARTS * 32, P // 32], [1, 32]])
                    sp.dma_start(q2nd[hh][STACK + part:STACK + part + 1, a * HALF:(a + 1) * HALF], rows
                                 ).then_inc(max_in[four], 16)

            def second_stacks(h, hh):
                sp.wait_ge(first_in[hh], (h - hh + 2) * 3 * 16)
                apart(sp, passed_sp)
                wait(sp, st_done, 2 * (h - 1) * EXPS)
                for to, of in ((q2nd[hh], q1st[hh]), (k2nd[hh], k1st[hh])):
                    sp.dma_start(to[0:STACK, :], of[:, :]).then_inc(second_in[hh], 16)

            sp.dma_start(w["w_out"][:, :, :], t["w_out"].rearrange("(k p) n -> p k n", p=P)).then_inc(out_in, 16)
            sp.dma_start(w["b_out"][:, :], bass.AP(tensor=t["b_out"].tensor, offset=0,
                                                   ap=[[0, P], [1, D]])).then_inc(out_in, 16)
            sp.dma_start(w["b_v_cols"][:, :], t["b_qkv_cols"][:, 2 * D // P:]).then_inc(out_in, 16)
            second_stacks(0, 0)
            for name in FFN:
                sp.dma_start(w[name][:, :, :].bitcast(I32), t[name].rearrange("(k p) n -> p k n", p=P)
                             ).then_inc(ffn_in, 16)
            maxima(0, 0, 0)

            def body(i, hh, first, last):
                h = 2 * i + hh
                if not first:
                    out["odd_rows"](sp, h - 1, 1)
                if not last:
                    second_stacks(h + 1, 1 - hh)
                if not first:
                    out["keep"](sp, h - 1, 1)
                    out["inverses"](sp, h - 1, 0)
                maxima(h, hh, 1)
                if last:
                    sp.wait_ge(v_ready, HEADS)
                    for at in range(2):
                        sp.wait_ge(kept[at], N_HEAD * QC * 16)
                        sp.wait_ge(inverses_out[at], N_HEAD * 16)
                    for c in range(2):
                        steps["load"](sp, c, c)
                if first:
                    for stored in s["stored"]:
                        sp.wait_ge(stored, B * (T // BANK // 2) * 16 * 2 * D // P)
                if not isinstance(i, int) or i < HEADS // 2 - 1:
                    sp.wait_ge(s_done, (h + 1) * 2 * MAXES)
                    sp.wait_ge(second_in[hh], (i + 1) * 2 * 16)
                    load_stacks(sp, t, h + 2, q1st[hh], k1st[hh], first_in[hh])
                out["odd_rows"](sp, h, 0)
                out["keep"](sp, h, 0)
                if not first:
                    out["inverses"](sp, h - 1, 1)
                if not last:
                    maxima(h + 1, 1 - hh, 0)

            each_head(sp, body)
            out["inverses"](sp, HEADS - 1, 0)
            for a in range(2):
                sp.wait_ge(kept[a], (HEADS - a) * QC * 16)
                sp.wait_ge(inverses_out[a], (HEADS - a) * 16)

        @block.tensor
        def _(pe):
            def pass_1(h, hh, a, r):
                qt, kw = a * QT + r // KW, r % KW
                wait(pe, s_read, (2 * h + a) * MAXES + r - 1)
                for j in range(2):
                    at = kw * WIDE + j * BANK
                    mm = pe.matmul(s_ps[r % 2][:, j * BANK:(j + 1) * BANK], q1st[hh][:, qt * P:(qt + 1) * P],
                                   k1st[hh][:, at:at + BANK], start=True, stop=True)
                mm.then_inc(s_done, 1)

            def pass_2(h, hh, a, kt, c):
                e = kt * QC + c
                if isinstance(h, int) and (h, a, e) == (0, 0, 0):
                    pe.wait_ge(bias_added, 1)
                wait(pe, exp_done, (2 * h + a) * EXPS + before(e, ST) + 1)
                at = a * HALF + c * BANK
                pe.matmul(st_ps[e % ST][:, :], k2nd[hh][:, kt * P:(kt + 1) * P], q2nd[hh][:, at:at + BANK],
                          start=True, stop=True).then_inc(st_done, 1)

            def times_v(h, hh, a, pair):
                u = 2 * h + a
                pe.wait_ge(exp_done, u * EXPS + (pair + 1) * 2 * QC)
                if pair == 0:
                    wait(pe, sums_out, u)
                for kk in range(2):
                    for c in range(QC):
                        at = (2 * kk + c) * 32
                        mm = pe.matmul(o_ps[at:at + VM, :], v_head[hh][:, 2 * pair + kk, :],
                                       probs[pair % SLOTS][:, kk, c * BANK:(c + 1) * BANK],
                                       start=pair == 0, stop=pair == PAIRS - 1, tile_position=(0, at))
                mm.then_inc(pv_done, 1)

            pe.wait_ge(first_in[0], 6 * 16)
            for r in range(MAXES):
                pass_1(0, 0, 0, r)
            pe.wait_ge(b_spread, D // P)
            pe.wait_ge(out_in, 3 * 16)
            for kd in range(D // P):
                mm = pe.matmul(st_ps[0][:, 0:D], w["b_v"][:, kd, :], w["w_out"][:, kd, :], start=kd == 0,
                               stop=kd == D // P - 1)
            mm.then_inc(bias_done, 1)
            for r in range(MAXES // 2):
                pass_1(0, 0, 1, r)
            pe.wait_ge(o_cleared, 1)
            pe.wait_ge(ones_set, 4)

            def body(i, hh, first, last):
                h = 2 * i + hh
                pe.wait_ge(second_in[hh], (i + 1) * 2 * 16)
                if not last:
                    pe.wait_ge(first_in[1 - hh], (i + hh + 1) * 6 * 16)
                for a in range(2):
                    pe.wait_ge(max_in[2 * hh + a], (i + 1) * PARTS * 16)
                    for p in range(PAIRS):
                        for kk in range(2):
                            for c in range(QC):
                                pass_2(h, hh, a, 2 * p + kk, c)
                            r = 2 * p + kk
                            if r < MAXES // 2 and a == 0:
                                pass_1(h, hh, 1, r + MAXES // 2)
                            elif r < MAXES // 2 and not last:
                                pass_1(h + 1, 1 - hh, 0, r + MAXES // 2)
                            elif r >= MAXES // 2 and not last:
                                pass_1(h + 1, 1 - hh, a, r - MAXES // 2)
                        if p > 0:
                            if p == 1 and a == 0:
                                pe.wait_ge(v_ready, h + 1)
                            times_v(h, hh, a, p - 1)
                        elif a == 1:
                            times_v(h, hh, 0, PAIRS - 1)
                        elif not first:
                            times_v(h - 1, 1 - hh, 1, PAIRS - 1)
                        if last and a == 1 and p >= PAIRS - TT:
                            if p == PAIRS - TT:
                                pe.wait_ge(s_read, 2 * HEADS * MAXES)
                            steps["output_projection"](pe, 0, 0, p_first, [p - PAIRS + TT])

            each_head(pe, body)
            times_v(HEADS - 1, 1, 1, PAIRS - 1)
            pe.wait_ge(topped, 2 * len(FFN) + 2)
            pe.matmul(s_ps[1][:, 0:1], w["ones"][:, :], w["wide"][:, :], start=True, stop=True
                      ).then_inc(f["wide_summed"], 1)

        @block.scalar
        def _(act):
            def body(i, hh, first, last):
                h = 2 * i + hh
                for a in range(2):
                    u = 2 * h + a
                    for e in range(EXPS):
                        pair, kk, c = e // (2 * QC), e // QC % 2, e % QC
                        if e % (2 * QC) == 0:
                            wait(act, pv_done, u * PAIRS + pair - SLOTS + 1)
                        act.wait_ge(st_done, u * EXPS + e + 1)
                        act.activation(probs[pair % SLOTS][:, kk, c * BANK:(c + 1) * BANK],
                                       st_ps[e % ST][:, :], ACT.Exp, scale=SCALE).then_inc(exp_done, 1)

            act.wait_ge(out_in, 3 * 16)
            act.wait_ge(all_ones, 1)
            for kd in range(D // P):
                act.activation(w["b_v"][:, kd, :], w["ones"][:, :], ACT.Identity,
                               scale=w["b_v_cols"][:, kd:kd + 1]).then_inc(b_spread, 1)
            act.wait_ge(ffn_in, len(FFN) * 16)
            for name in FFN:
                act.copy(w[name][:, :, :], w[name][:, :, :].bitcast(I32)).then_inc(floats, 1)
            each_head(act, body)
            steps["deviations"](act, 0)
            act.wait_ge(f["wide_summed"], 1)
            act.copy(f["wide_count"][:, :], s_ps[1][:, 0:1]).then_inc(f["wide_known"], 1)
            act.wait_ge(f["wide_known"], 1)
            act.copy(f["wide_int"][:, :], f["wide_count"][0:1, :]).then_inc(f["wide_known"], 1)

        @block.vector
        def _(dve):
            dve.memset(o_ps[:, :], 0.0).then_inc(o_cleared, 1)
            for a in range(2):
                dve.memset(neg_max[a][:, :], 0.0).then_inc(cleared, 1)
            dve.wait_ge(cleared, 2)

            def maximum(h, a, r):
                u = 2 * h + a
                if r == 0:
                    wait(dve, unit_max, u - 1)
                dve.wait_ge(s_done, u * MAXES + r + 1)
                dve.tensor_reduce(tile_max[a][:, r // KW, r % KW:r % KW + 1], s_ps[r % 2][:, :],
                                  AX.X, ALU.max).then_inc(s_read, 1)

            def unit_maxima(h, a):
                u = 2 * h + a
                dve.wait_ge(s_read, (u + 1) * MAXES)
                wait(dve, max_turned, u - 1)
                dve.tensor_reduce(neg_max[a][:, 0:QT], tile_max[a][:, :, :], AX.X, ALU.max,
                                  negate=True).then_inc(unit_max, 1)
                dve.wait_ge(unit_max, u + 1)
                wait(dve, max_cut, CUTS * (u - 1))
                dve.transpose(neg_max_t[a][:, :], neg_max[a][:, :]).then_inc(max_turned, 1)

            for r in range(MAXES):
                maximum(0, 0, r)
            unit_maxima(0, 0)
            dve.wait_ge(bias_done, 1)
            dve.tensor_tensor(w["b_out"][:, :], st_ps[0][:, 0:D], w["b_out"][:, :], ALU.add
                              ).then_inc(bias_added, 1)
            for r in range(MAXES // 2):
                maximum(0, 1, r)

            def drain(h, a):
                u = 2 * h + a
                dve.wait_ge(pv_done, (u + 1) * PAIRS)
                wait(dve, whole_done, u - 1)
                dve.tensor_copy(sums[a][:, :], o_ps[:, :]).then_inc(sums_out, 1)

            def halve_weights():
                dve.wait_ge(floats, len(FFN))
                for name in FFN:
                    dve.tensor_scalar(w[name + "_half"][:, :, :], w[name][:, :, :], float(NARROW), float(-NARROW),
                                      ALU.min, ALU.max)

            def flag_wide():
                for n, name in enumerate(FFN):
                    for low in range(2):
                        dve.tensor_reduce(tops[:, 2 * n + low:2 * n + low + 1], w[name][:, :, :], AX.XY,
                                          ALU.min if low else ALU.max, negate=bool(low)).then_inc(topped, 1)
                dve.wait_ge(topped, 2 * len(FFN))
                dve.tensor_reduce(top[:, :], tops[:, :], AX.X, ALU.max).then_inc(topped, 1)
                dve.wait_ge(topped, 2 * len(FFN) + 1)
                dve.tensor_scalar(w["wide"][:, :], top[:, :], NARROW + 0.5, None, ALU.is_gt).then_inc(topped, 1)

            def body(i, hh, first, last):
                h = 2 * i + hh
                for a in range(2):
                    h_before, a_before = (h, 0) if a == 1 else (h - 1, 1)
                    any_before = a == 1 or not first
                    for r in range(MAXES // 2):
                        if a == 0:
                            maximum(h, 1, r + MAXES // 2)
                        elif not last:
                            maximum(h + 1, 0, r + MAXES // 2)
                        if any_before and r == 1:
                            drain(h_before, a_before)
                    if a == 0:
                        unit_maxima(h, 1)
                    elif not last:
                        unit_maxima(h + 1, 0)
                    for r in range(MAXES // 2):
                        if not last:
                            maximum(h + 1, a, r)
                        elif r == 0 and a == 0:
                            halve_weights()
                        elif r == 0:
                            flag_wide()
                        if any_before and r == MAXES // 4:
                            out["invert"](dve, h_before, a_before)

            each_head(dve, body)
            dve.memset(f["moments"][:, :, :], 1.0).then_inc(f["z_moments"], 1)
            steps["sum_z"](dve, 0, 0, p_first)
            steps["count_z"](dve, 0)
            steps["average_z"](dve, 0)
            steps["variances"](dve, 0, 1, 0)
            drain(HEADS - 1, 1)
            steps["invert"](dve, 0, 0, 0)
            steps["normalize"](dve, f["x1"][0], f["z"], 0, f["x1_done"])
            dve.wait_ge(f["wide_known"], 1)
            dve.tensor_scalar(f["hidden_factor"][:, :], f["wide_count"][:, :], 0.0, WIDE_SCALE,
                              ALU.is_equal, ALU.max).then_inc(f["factors"], 1)
            dve.tensor_scalar(f["down_factor"][:, :], f["wide_count"][:, :], 0.0, 1 / WIDE_SCALE,
                              ALU.is_gt, ALU.mult).then_inc(f["factors"], 1)
            dve.wait_ge(f["factors"], 2)
            dve.tensor_scalar(f["hidden_factor"][:, :], f["hidden_factor"][:, :],
                              QUANT_SCALE / X1_SCALE * HIDDEN_SCALE, None, ALU.mult).then_inc(f["factors"], 1)
            dve.tensor_scalar(f["down_factor"][:, :], f["down_factor"][:, :], 1.0, QUANT_SCALE / HIDDEN_SCALE,
                              ALU.max, ALU.mult).then_inc(f["factors"], 1)
            dve.wait_ge(f["factors"], 4)

        @block.gpsimd
        def _(pool):
            pool.memset(w["ones"][:, :], 1.0).then_inc(all_ones, 1)
            pool.wait_ge(all_ones, 1)
            for i in range(2):
                wait(pool, ones_set, 2 * i)
                pool.memset(k2nd[i][STACK:ROWS, :], 1.0).then_inc(ones_set, 1)
                pool.wait_ge(ones_set, 2 * i + 1)
                pool.memset(v_head[i][:, :, HD:VM], 1.0).then_inc(ones_set, 1)
            pool.wait_ge(ones_set, 4)

            def cut(h, a):
                steps = CUTS * (2 * h + a)
                pool.wait_ge(max_turned, 2 * h + a + 1)
                wait(pool, max_out[a], h * 16)
                apart(pool, passed_pool)
                pool.tensor_copy(max_parts[a][:, 0, :], neg_max_t[a][:, :]).then_inc(max_cut, 1)
                pool.wait_ge(max_cut, steps + 1)
                pool.tensor_tensor(max_rest[:, :], neg_max_t[a][:, :], max_parts[a][:, 0, :],
                                   ALU.subtract).then_inc(max_cut, 1)
                pool.wait_ge(max_cut, steps + 2)
                apart(pool, passed_pool)
                pool.tensor_copy(max_parts[a][:, 1, :], max_rest[:, :]).then_inc(max_cut, 1)
                pool.wait_ge(max_cut, steps + 3)
                pool.tensor_tensor(max_parts[a][:, 2, :], max_rest[:, :], max_parts[a][:, 1, :],
                                   ALU.subtract).then_inc(max_cut, 1)

            def head_v(h, hh):
                wait(pool, pv_done, (h - 1) * 2 * PAIRS)
                apart(pool, passed_pool)
                pool.tensor_copy(v_head[hh][:, :, 0:HD],
                                 t["kept"][:, bass.ds(h, 1), :, :].rearrange("p h k d -> p (h k) d")
                                 ).then_inc(v_ready, 1)

            head_v(0, 0)
            cut(0, 0)
            pool.memset(w["ident"][:, :], 0.0).then_inc(ident_set, 1)
            pool.wait_ge(ident_set, 1)
            pool.affine_select(out=w["ident"][:, :], in_=w["ident"][:, :], compare_op=ALU.not_equal, fill=1.0,
                               base=0, pattern=[[-1, P]], channel_multiplier=1)

            def body(i, hh, first, last):
                h = 2 * i + hh
                if not first:
                    out["add_odd"](pool, h - 1, 1)
                if not last:
                    head_v(h + 1, 1 - hh)
                cut(h, 1)
                if last:
                    pool.wait_ge(bias_added, 1)
                    for c in range(2):
                        steps["divide"](pool, c, c)
                        steps["bias"](pool, c, c)
                out["add_odd"](pool, h, 0)
                if not last:
                    cut(h + 1, 0)

            each_head(pool, body)


def finish(nc, t, w, f, u, B, T, D, HID):
    CH = BANK
    NCS = T // CH
    NCH = B * NCS
    TT = CH // P
    KD = D // P
    HD = D // N_HEAD
    HPT = P // HD
    HT = HID // P
    with ExitStack() as ctx:
        def sb(name, shape, dt=F32):
            return ctx.enter_context(nc.sbuf_tensor(name, shape, dt))

        def psum(name, shape):
            return ctx.enter_context(nc.psum_tensor(name, shape, F32))

        def sem(name):
            return ctx.enter_context(nc.semaphore(name))

        steps = norm_steps(nc, t, w, f, B, T, D)
        out = unit_steps(t, u, T, D)
        HEADS = B * N_HEAD
        landed, x1 = steps["landed"], f["x1"]
        x1_t = sb("x1_t", [P, KD, CH])
        x1_high = sb("x1_high", [P, KD, CH], F16)
        x1_low = sb("x1_low", [P, KD, CH], F16)
        silu = [sb(f"silu{i}", [P, CH]) for i in range(2)]
        hidden = sb("hidden", [P, HT, CH])
        h_high = sb("h_high", [P, HT, CH], F16)
        h_low = sb("h_low", [P, HT, CH], F16)
        y = [sb(f"y{i}", [P, TT, D]) for i in range(2)]
        result = [sb(f"result{i}", [P, TT, D]) for i in range(2)]
        warm = sb("warm", [P, 1])

        t_ps = psum("t_ps", [P, KD, CH])
        p_ps = psum("p_ps", [P, TT, D])
        g_ps = [psum(f"g_ps{i}", [P, CH]) for i in range(2)]
        u_ps = [psum(f"u_ps{i}", [P, CH]) for i in range(2)]

        turned = sem("turned")
        x1_high_done = sem("x1_high_done")
        x1_low_done = sem("x1_low_done")
        x1_t_done = sem("x1_t_done")
        gate_done = sem("gate_done")
        up_done = sem("up_done")
        silu_done = sem("silu_done")
        hidden_done = sem("hidden_done")
        h_high_done = sem("h_high_done")
        h_low_done = sem("h_low_done")
        last_low_done = sem("last_low_done")
        down_done = sem("down_done")
        y_done, y_moments, result_done = f["y_done"], f["y_moments"], f["result_done"]
        x1_done, z_done = f["x1_done"], f["z_done"]
        y_stats = sem("y_stats")
        kept = [sem(f"result_kept{i}") for i in range(2)]

        def each_chunk(eng, body):
            def turn(i, first, last):
                body(2 * i, 0, first, False)
                body(2 * i + 1, 1, False, last)
            turn(0, True, False)
            with eng.Fori(1, NCH // 2 - 1) as i:
                turn(i, False, False)
            turn(NCH // 2 - 1, False, True)

        block = ctx.enter_context(nc.Block())

        @block.sync
        def _(sp):
            def body(c, par, first, last):
                if not isinstance(c, int) or c + 2 < NCH:
                    steps["load"](sp, c + 2, par)
                if first:
                    out["inverses"](sp, HEADS - 1, 1)
                    sp.wait_ge(u["kept"][1], HEADS * (T // 2 // BANK) * 16)
                    sp.wait_ge(u["inverses_out"][1], HEADS * 16)
                if not first and (not isinstance(c, int) or c > 1):
                    keep(c - 2, par)

            def keep(c, par):
                sp.wait_ge(result_done, c + 1)
                sp.dma_start(t["out"].rearrange("(n p) d -> p n d", p=P)[:, bass.ds(c * TT, TT), :],
                             result[par][:, :, :]).then_inc(kept[par], 16)

            out["odd_rows"](sp, HEADS - 1, 1)
            out["keep"](sp, HEADS - 1, 1)
            each_chunk(sp, body)
            keep(NCH - 2, 0)
            keep(NCH - 1, 1)
            for par in range(2):
                sp.wait_ge(kept[par], NCH // 2 * 16)

        @block.tensor
        def _(pe):
            def ffn(wide):
                def product(to, pairs, first, last):
                    for n, (stationary, moving) in enumerate(pairs):
                        mm = pe.matmul(to, stationary, moving, start=first and n == 0,
                                       stop=last and n == len(pairs) - 1)
                    return mm

                def project_in(name, to, m):
                    for kd in range(KD):
                        at = (slice(None), kd, slice(m * P, (m + 1) * P))
                        if wide:
                            pairs = [(w[name][at], x1_t[:, kd, :])]
                        else:
                            half = w[name + "_half"][at]
                            pairs = [(half, x1_high[:, kd, :]), (half, x1_low[:, kd, :])]
                        mm = product(to, pairs, kd == 0, kd == KD - 1)
                    return mm

                def body(c, par, first, last):
                    pe.wait_ge(x1_done, c + 1)
                    wait(pe, x1_t_done, KD * c)
                    for kd in range(KD):
                        for n in range(TT):
                            mm = pe.transpose(t_ps[:, kd, n * P:(n + 1) * P], x1[par][:, n, kd * P:(kd + 1) * P],
                                              w["ident"][:, :])
                        mm.then_inc(turned, 1)
                    if not last:
                        steps["output_projection"](pe, c + 1, 1 - par, p_ps)
                    pe.wait_ge(x1_low_done, KD * (c + 1))
                    for m in range(HT):
                        wait(pe, silu_done, c * HT + m - 1)
                        project_in("w_gate", g_ps[m % 2][:, :], m).then_inc(gate_done, 1)
                        wait(pe, hidden_done, c * HT + m - 1)
                        project_in("w_up", u_ps[m % 2][:, :], m).then_inc(up_done, 1)
                    if not last:
                        pe.wait_ge(z_done, 2 * (c + 2))
                    for tiles in ((0, TT // 2), (1,), (TT // 2 + 1,)):
                        for m in range(HT):
                            if tiles[0] == 0:
                                if m < HT - 1:
                                    pe.wait_ge(h_low_done, c * (HT - 1) + m + 1)
                                else:
                                    pe.wait_ge(last_low_done, c + 1)
                            for n in tiles:
                                at = (slice(None), m, slice(n * P, (n + 1) * P))
                                if wide:
                                    pairs = [(hidden[at], w["w_down"][:, m, :])]
                                else:
                                    half = w["w_down_half"][:, m, :]
                                    pairs = [(h_high[at], half), (h_low[at], half)]
                                mm = product(p_ps[:, n, :], pairs, m == 0, m == HT - 1)
                        if tiles[0] > 0:
                            mm.then_inc(down_done, 1)

                each_chunk(pe, body)

            wide = pe.value_load(f["wide_int"][0:1, 0:1], min_val=0, max_val=P)
            with pe.If(wide > 0):
                ffn(True)
            with pe.Else():
                ffn(False)

        @block.scalar
        def _(act):
            def load_silu():
                act.activation(warm[:, :], w["ones"][:, 0:1], ACT.Silu)

            def high(c, m):
                act.wait_ge(hidden_done, c * HT + m + 1)
                if m < HT - 1:
                    wait(act, h_low_done, (c - 1) * (HT - 1) + m + 1)
                else:
                    wait(act, last_low_done, c)
                act.copy(h_high[:, m, :], hidden[:, m, :]).then_inc(h_high_done, 1)

            load_silu()

            def body(c, par, first, last):
                for kd in range(KD):
                    act.wait_ge(turned, KD * c + kd + 1)
                    act.activation(x1_t[:, kd, :], t_ps[:, kd, :], ACT.Copy, scale=X1_SCALE
                                   ).then_inc(x1_t_done, 1)
                    act.wait_ge(x1_t_done, KD * c + kd + 1)
                    act.copy(x1_high[:, kd, :], x1_t[:, kd, :]).then_inc(x1_high_done, 1)
                for m in range(HT):
                    act.wait_ge(gate_done, c * HT + m + 1)
                    wait(act, hidden_done, c * HT + m - 1)
                    act.activation(silu[m % 2][:, :], g_ps[m % 2][:, :], ACT.Silu,
                                   scale=QUANT_SCALE / X1_SCALE).then_inc(silu_done, 1)
                    if m > 0:
                        high(c, m - 1)
                high(c, HT - 1)
                steps["deviations"](act, c + 1)
                if not last:
                    load_silu()

            each_chunk(act, body)
            steps["deviations"](act, NCH + 1)

        @block.vector
        def _(dve):
            def sum_y(c, par):
                for j in range(2):
                    dve.wait_ge(down_done, 2 * c + j + 1)
                    if j == 0:
                        wait(dve, result_done, c - 1)
                    dve.scalar_tensor_tensor(y[par][:, 2 * j:2 * j + 2, :], p_ps[:, 2 * j:2 * j + 2, :],
                                             f["down_factor"][:, 0:1], x1[par][:, 2 * j:2 * j + 2, :],
                                             ALU.mult, ALU.add).then_inc(y_done, 1)

            def moments_y(c, par):
                dve.wait_ge(y_done, 2 * c + 2)
                wait(dve, y_moments, TT * c)
                wait(dve, f["var_done"], c + 2)
                wait(dve, result_done, c)
                steps["count"](dve, y[par], TT, y_stats)
                steps["average"](dve, TT, c, y_stats, y_moments)

            def hide(c, m):
                dve.wait_ge(silu_done, c * HT + m + 1)
                dve.wait_ge(up_done, c * HT + m + 1)
                if m < HT - 1:
                    wait(dve, h_low_done, (c - 1) * (HT - 1) + m + 1)
                else:
                    wait(dve, last_low_done, c)
                dve.scalar_tensor_tensor(hidden[:, m, :], u_ps[m % 2][:, :],
                                         f["hidden_factor"][:, 0:1], silu[m % 2][:, :],
                                         ALU.mult, ALU.mult).then_inc(hidden_done, 1)

            def low_hidden(c):
                dve.wait_ge(h_high_done, (c + 1) * HT)
                dve.tensor_tensor(h_low[:, HT - 1, :], hidden[:, HT - 1, :], h_high[:, HT - 1, :],
                                  ALU.subtract).then_inc(last_low_done, 1)

            def low(c, kd):
                dve.wait_ge(x1_high_done, KD * c + kd + 1)
                dve.tensor_tensor(x1_low[:, kd, :], x1_t[:, kd, :], x1_high[:, kd, :],
                                  ALU.subtract).then_inc(x1_low_done, 1)

            def second_norm(c, par):
                wait(dve, kept[par], landed(c, par) - 16)
                steps["normalize"](dve, result[par], y[par], TT, result_done)

            def body(c, par, first, last):
                if not first:
                    sum_y(c - 1, 1 - par)
                for kd in range(KD):
                    low(c, kd)
                if not first:
                    if not isinstance(c, int) or c > 1:
                        second_norm(c - 2, par)
                    moments_y(c - 1, 1 - par)
                hide(c, 0)
                if not last:
                    steps["sum_z"](dve, c + 1, 1 - par, p_ps)
                if first:
                    out["invert"](dve, HEADS - 1, 1)
                hide(c, 1)
                if not last:
                    steps["count_z"](dve, c + 1)
                hide(c, 2)
                if not last:
                    steps["average_z"](dve, c + 1)
                steps["variances"](dve, c + 1, NCH if last else c + 2, c)
                for m in range(3, HT):
                    hide(c, m)
                low_hidden(c)
                steps["invert"](dve, c + 1, c + 1, c - 1)
                if not last:
                    steps["normalize"](dve, x1[1 - par], f["z"], 0, x1_done)

            each_chunk(dve, body)
            sum_y(NCH - 1, 1)
            second_norm(NCH - 2, 0)
            moments_y(NCH - 1, 1)
            steps["variances"](dve, NCH + 1, NCH, NCH)
            steps["invert"](dve, NCH + 1, NCH, NCH - 1)
            second_norm(NCH - 1, 1)

        @block.gpsimd
        def _(pool):
            def body(c, par, first, last):
                if not isinstance(c, int) or c + 2 < NCH:
                    steps["divide"](pool, c + 2, par)
                    steps["bias"](pool, c + 2, par)
                for m in range(HT - 1):
                    pool.wait_ge(h_high_done, c * HT + m + 1)
                    pool.tensor_tensor(h_low[:, m, :], hidden[:, m, :], h_high[:, m, :],
                                       ALU.subtract).then_inc(h_low_done, 1)

            out["add_odd"](pool, HEADS - 1, 1)
            each_chunk(pool, body)


def layer(nc, t, B, T, D, HID):
    HD = D // N_HEAD
    HEADS = B * N_HEAD
    t["q_parts"] = nc.dram_tensor("q_parts", [HEADS, HD, PARTS, T], BF16).ap()
    t["k_parts"] = nc.dram_tensor("k_parts", [HEADS, HD, PARTS, T], BF16).ap()
    t["max_parts"] = nc.dram_tensor("max_parts_out", [4, P, PARTS, 32], BF16).ap()
    t["heads"] = nc.dram_tensor("heads_out", [HEADS * HD, T], F32).ap()
    t["inverses"] = nc.dram_tensor("inverses_out", [HEADS, T], F32).ap()
    with ExitStack() as ctx:
        def sb(name, shape, dt=F32):
            return ctx.enter_context(nc.sbuf_tensor(name, shape, dt))

        t["kept"] = sb("kept_v", [P, HEADS, T // P, HD])
        s = {name: [sb(f"{name}{i}", [6 * HD, T], BF16) for i in range(2)] for name in ("q1st", "k1st")}
        s["parts"] = [sb(f"parts{i}", [P, 2 * D // P, PARTS, BANK], BF16) for i in range(2)]
        s["stored"] = [ctx.enter_context(nc.semaphore(f"stored{i}")) for i in range(2)]
        s["first_in"] = [ctx.enter_context(nc.semaphore(f"first_in{i}")) for i in range(2)]
        project(nc, t, s, B, T, D)

        w = {"w_out": sb("w_out", [P, D // P, D]), "b_out": sb("b_out", [P, D]),
             "b_v": sb("b_v", [P, D // P, P]), "b_v_cols": sb("b_v_cols", [P, D // P]),
             "ident": sb("ident", [P, P]), "ones": sb("ones", [P, P]),
             "wide": sb("wide", [P, 1])}
        for name, rows, columns in (("w_gate", D, HID), ("w_up", D, HID), ("w_down", HID, D)):
            w[name] = sb(name, [P, rows // P, columns])
            w[name + "_half"] = sb(name + "_half", [P, rows // P, columns], F16)
        f = norm_state(ctx, nc, t, B, T, D)
        u = unit_state(ctx, nc, T)
        attend(nc, t, w, s, f, u, B, T, D)
        finish(nc, t, w, f, u, B, T, D, HID)


def rotary_tables(T, hd, rows):
    inv = (np.float32(1.0) / np.float32(10000.0) ** (np.arange(0, hd, 2, dtype=np.float32) / np.float32(hd)))
    angle = np.repeat(np.arange(T, dtype=np.float32)[:, None] * inv.astype(np.float32)[None, :], 2, axis=1).T
    sign = np.where(np.arange(hd) % 2 == 0, -1.0, 1.0).astype(np.float32)[:, None]
    return (np.ascontiguousarray(np.tile(np.cos(angle), (rows // hd, 1)), np.float32),
            np.ascontiguousarray(np.tile(np.sin(angle) * sign, (rows // hd, 1)), np.float32))


def kernel(L0_attn_x, L0_attn_w_qkv, L0_attn_b_qkv, L0_attn_w_out, L0_attn_b_out,
           L0_ffn_w_gate, L0_ffn_w_up, L0_ffn_w_down):
    import concourse.bacc as bacc
    from concourse.bass_utils import run_bass_kernel_spmd

    x = np.asarray(L0_attn_x)
    B, T, D = x.shape
    HID = L0_ffn_w_gate.shape[0]
    cos, sin = rotary_tables(T, D // N_HEAD, P)
    flat = x.reshape(B * T, D)
    arrays = {
        "x": np.ascontiguousarray(flat),
        "x_t": np.ascontiguousarray(flat.T),
        "w_qkv": np.ascontiguousarray(L0_attn_w_qkv),
        "b_qkv_cols": np.ascontiguousarray(np.asarray(L0_attn_b_qkv).reshape(3 * D // P, P).T),
        "w_out": np.ascontiguousarray(L0_attn_w_out),
        "b_out": np.ascontiguousarray(L0_attn_b_out),
        "w_gate": np.ascontiguousarray(np.asarray(L0_ffn_w_gate).T),
        "w_up": np.ascontiguousarray(np.asarray(L0_ffn_w_up).T),
        "w_down": np.ascontiguousarray(np.asarray(L0_ffn_w_down).T),
        "cos": cos,
        "sin": sin,
    }
    nc = bacc.Bacc("TRN2", target_bir_lowering=False, num_devices=1)
    t = {n: nc.dram_tensor("in_" + n, a.shape, mybir.dt.from_np(a.dtype), kind="ExternalInput").ap()
         for n, a in arrays.items()}
    t["out"] = nc.dram_tensor("out", (B * T, D), F32, kind="ExternalOutput").ap()
    layer(nc, t, B, T, D, HID)
    r = run_bass_kernel_spmd(nc, [{"in_" + n: a for n, a in arrays.items()}], core_ids=[0])
    return r.results[0]["out"].reshape(B, T, D)
```
